# Optimizing a Trainium2 kernel written in Bass

```python
import numpy as np
import jax
import jax.numpy as jnp

def _softmax(x, axis=-1):
    return jax.nn.softmax(x, axis=axis)

def _gelu(x):
    return jax.nn.gelu(x, approximate=True)

def _silu(x):
    return jax.nn.silu(x)

def _sigmoid(x):
    return jax.nn.sigmoid(x)

def _layernorm(x, axis=-1, eps=1e-05):
    m = jnp.mean(x, axis=axis, keepdims=True)
    v = jnp.var(x, axis=axis, keepdims=True)
    return (x - m) / jnp.sqrt(v + eps)

def _scatter_add(tgt, idx, src, axis=0):
    return tgt.at[idx].add(src)

def _segment_sum(src, seg, n):
    return jax.ops.segment_sum(src, seg, n)
kernel_name = 'mk_gnn_resnorm_d2_gnn_r16_b51d02'

def setup_inputs(seed: int=0):
    np.random.seed(seed)
    _w = jnp.asarray

    def _rec_inputs():
        import jax
        import jax.numpy as jnp
        _gk = jax.random.key(seed)
        x = -0.0009044 + 1 * jax.random.normal(jax.random.fold_in(_gk, 1), (6250, 32), jnp.float32)
        _s = jax.random.randint(jax.random.fold_in(_gk, 2), (50000,), 0, 6250, jnp.int32)
        _d = jax.random.randint(jax.random.fold_in(_gk, 3), (50000,), 0, 6250, jnp.int32)
        _loop = jnp.arange(6250, dtype=jnp.int32)
        src = jnp.concatenate([_s, _d, _loop])
        dst = jnp.concatenate([_d, _s, _loop])
        _o = jnp.argsort(dst, stable=True)
        src = src[_o]
        dst = dst[_o]
        edge_attr_3 = 0.000844983 + 0.999762 * jax.random.normal(jax.random.fold_in(_gk, 11), (106250, 3), jnp.float32)
        edge_weight = jax.random.uniform(jax.random.fold_in(_gk, 13), (106250,), jnp.float32, 0.0, 1)
        edge_weight1 = 0.000614103 + 0.999867 * jax.random.normal(jax.random.fold_in(_gk, 14), (106250, 1), jnp.float32)
        return (x, src, dst, edge_attr_3, edge_weight, edge_weight1)
    x, src, dst, edge_attr_3, edge_weight, edge_weight1 = _rec_inputs()

    def _L0_gnn_setup():
        import jax, jax.numpy as jnp
        import numpy as np
        N = 3125
        E = 50000
        H = 8
        C = 32
        L = 3
        NEG_SLOPE = 0.2
        BN_EPS = 1e-05

        def gatv2_layer(x, Wl, bl, Wr, br, att, bias, src, dst, n):
            xl = (x @ Wl + bl).reshape(n, H, C)
            xr = (x @ Wr + br).reshape(n, H, C)
            e = jax.nn.leaky_relu(xl[src] + xr[dst], NEG_SLOPE)
            logits = jnp.einsum('ehc,hc->eh', e, att)
            m = jax.ops.segment_max(logits, dst, num_segments=n)
            m = jnp.where(jnp.isfinite(m), m, 0.0)
            p = jnp.exp(logits - jax.lax.stop_gradient(m)[dst])
            denom = jax.ops.segment_sum(p, dst, num_segments=n)
            alpha = p / (denom[dst] + 1e-16)
            out = jax.ops.segment_sum(xl[src] * alpha[:, :, None], dst, num_segments=n)
            return out.mean(axis=1) + bias

        def batchnorm_train(x, gamma, beta):
            mu = x.mean(axis=0)
            var = x.var(axis=0)
            return (x - mu) * jax.lax.rsqrt(var + BN_EPS) * gamma + beta
        key = jax.random.key(seed)
        ks = jax.random.split(key, 8)
        s = 1.0 / np.sqrt(C)
        return {'patch_embs': jax.random.normal(ks[0], (N, C), jnp.float32), 'edge_index': jax.random.randint(ks[1], (2, E), 0, N, dtype=jnp.int32), 'edge_attr': jax.random.normal(ks[2], (E, 1), jnp.float32), 'Wl': jax.random.normal(ks[3], (L, C, H * C), jnp.float32) * s, 'bl': jnp.zeros((L, H * C), jnp.float32), 'Wr': jax.random.normal(ks[4], (L, C, H * C), jnp.float32) * s, 'br': jnp.zeros((L, H * C), jnp.float32), 'att': jax.random.normal(ks[5], (L, H, C), jnp.float32) * s, 'conv_bias': jnp.zeros((L, C), jnp.float32), 'bn_gamma': jnp.ones((L, C), jnp.float32), 'bn_beta': jnp.zeros((L, C), jnp.float32)}
    _L0_gnn_all = _L0_gnn_setup()
    _L0_gnn_in = {k: v for k, v in _L0_gnn_all.items() if k in ('Wl', 'bl', 'Wr', 'br', 'att', 'conv_bias', 'bn_gamma', 'bn_beta')}
    del _L0_gnn_all

    def _L1_gnn_setup():
        import jax, jax.numpy as jnp
        import numpy as np
        from math import factorial, pi, sqrt
        MUL = 8
        RS = [(MUL, 0), (MUL, 1)]
        N_NODES = 1250
        N_EDGES = 40000
        FEAT_DIM = sum((m * (2 * l + 1) for m, l in RS))
        R_DIM = sum((mo * mi * (2 * min(lo, li) + 1) for mo, lo in RS for mi, li in RS))
        HIDDEN = 64

        def _cg(j1, j2, j3, m1, m2, m3):
            if m1 + m2 != m3:
                return 0.0
            f = factorial
            pre = sqrt((2 * j3 + 1) * f(j3 + j1 - j2) * f(j3 - j1 + j2) * f(j1 + j2 - j3) / f(j1 + j2 + j3 + 1))
            pre *= sqrt(f(j3 + m3) * f(j3 - m3) * f(j1 - m1) * f(j1 + m1) * f(j2 - m2) * f(j2 + m2))
            kmin = max(0, j2 - j3 - m1, j1 - j3 + m2)
            kmax = min(j1 + j2 - j3, j1 - m1, j2 + m2)
            s = 0.0
            for k in range(kmin, kmax + 1):
                s += (-1) ** k / (f(k) * f(j1 + j2 - j3 - k) * f(j1 - m1 - k) * f(j2 + m2 - k) * f(j3 - j2 + m1 + k) * f(j3 - j1 - m2 + k))
            return pre * s

        def _w3j_complex(l1, l2, l3):
            w = np.zeros((2 * l1 + 1, 2 * l2 + 1, 2 * l3 + 1))
            for m1 in range(-l1, l1 + 1):
                for m2 in range(-l2, l2 + 1):
                    m3 = -(m1 + m2)
                    if abs(m3) <= l3:
                        w[m1 + l1, m2 + l2, m3 + l3] = (-1) ** (l1 - l2 - m3) / sqrt(2 * l3 + 1) * _cg(l1, l2, l3, m1, m2, -m3)
            return w

        def _A(l):
            A = np.zeros((2 * l + 1, 2 * l + 1), dtype=complex)
            A[l, l] = 1.0
            for m in range(1, l + 1):
                A[l + m, l + m] = (-1) ** m / sqrt(2)
                A[l + m, l - m] = 1.0 / sqrt(2)
                A[l - m, l - m] = 1j / sqrt(2)
                A[l - m, l + m] = -1j * (-1) ** m / sqrt(2)
            return A

        def real_w3j(l1, l2, l3):
            wc = _w3j_complex(l1, l2, l3).astype(complex)
            wr = np.einsum('abc,ma,nb,oc->mno', wc, _A(l1).conj(), _A(l2).conj(), _A(l3).conj())
            i = int(np.argmax(np.abs(wr)))
            ph = wr.flat[i] / abs(wr.flat[i])
            wr = wr / ph
            assert np.abs(wr.imag).max() < 1e-10
            return np.real(wr).astype(np.float32)
        _W3J = {}
        for _mo, _lo in RS:
            for _mi, _li in RS:
                for _lf in range(abs(_lo - _li), _lo + _li + 1):
                    if (_lo, _lf, _li) not in _W3J:
                        _W3J[_lo, _lf, _li] = jnp.asarray(real_w3j(_lo, _lf, _li))
        _NORM = []
        for _mo, _lo in RS:
            _num = sum((mi * (2 * min(_lo, li) + 1) for mi, li in RS))
            _NORM.append(sqrt(4.0 * pi) * sqrt(2.0 * _lo + 1.0) / sqrt(_num))
        _F_OFFS = [0] + list(np.cumsum([mi * (2 * li + 1) for mi, li in RS]))

        def spherical_harmonics(rel_vec):
            r = rel_vec / jnp.linalg.norm(rel_vec, axis=-1, keepdims=True)
            x, y, z = (r[:, 0], r[:, 1], r[:, 2])
            y0 = jnp.full_like(x, 0.5 / sqrt(pi))[:, None]
            c1 = sqrt(3.0 / (4.0 * pi))
            y1 = c1 * jnp.stack([y, z, x], axis=-1)
            c2a = 0.5 * sqrt(15.0 / pi)
            c2b = 0.25 * sqrt(5.0 / pi)
            c2c = 0.25 * sqrt(15.0 / pi)
            y2 = jnp.stack([c2a * x * y, c2a * y * z, c2b * (3.0 * z * z - 1.0), c2a * x * z, c2c * (x * x - y * y)], axis=-1)
            return jnp.concatenate([y0, y1, y2], axis=-1)
        key = jax.random.key(seed)
        ks = jax.random.split(key, 6)
        features = jax.random.normal(ks[0], (N_NODES, FEAT_DIM), dtype=jnp.float32)
        abs_distances = jax.random.uniform(ks[1], (N_EDGES,), dtype=jnp.float32, minval=0.1, maxval=1.0)
        rel_vec = jax.random.normal(ks[2], (N_EDGES, 3), dtype=jnp.float32)
        edge_index = jax.random.randint(ks[3], (2, N_EDGES), 0, N_NODES, dtype=jnp.int32)
        w1 = jax.random.normal(ks[4], (1, HIDDEN), dtype=jnp.float32)
        b1 = jnp.zeros((HIDDEN,), jnp.float32)
        w2 = jax.random.normal(ks[5], (HIDDEN, R_DIM), dtype=jnp.float32) / sqrt(HIDDEN)
        b2 = jnp.zeros((R_DIM,), jnp.float32)
        return {'features': features, 'abs_distances': abs_distances, 'rel_vec': rel_vec, 'edge_index': edge_index, 'w1': w1, 'b1': b1, 'w2': w2, 'b2': b2}
    _L1_gnn_all = _L1_gnn_setup()
    _L1_gnn_in = {k: v for k, v in _L1_gnn_all.items() if k in ('w1', 'b1', 'w2', 'b2')}
    del _L1_gnn_all
    return {'x': x, 'src': src, 'dst': dst, 'edge_attr_3': edge_attr_3, 'edge_weight': edge_weight, 'edge_weight1': edge_weight1, 'L0_gnn_Wl': _L0_gnn_in['Wl'], 'L0_gnn_bl': _L0_gnn_in['bl'], 'L0_gnn_Wr': _L0_gnn_in['Wr'], 'L0_gnn_br': _L0_gnn_in['br'], 'L0_gnn_att': _L0_gnn_in['att'], 'L0_gnn_conv_bias': _L0_gnn_in['conv_bias'], 'L0_gnn_bn_gamma': _L0_gnn_in['bn_gamma'], 'L0_gnn_bn_beta': _L0_gnn_in['bn_beta'], 'L1_gnn_w1': _L1_gnn_in['w1'], 'L1_gnn_b1': _L1_gnn_in['b1'], 'L1_gnn_w2': _L1_gnn_in['w2'], 'L1_gnn_b2': _L1_gnn_in['b2']}

def reference(x, src, dst, edge_attr_3, edge_weight, edge_weight1, L0_gnn_Wl, L0_gnn_bl, L0_gnn_Wr, L0_gnn_br, L0_gnn_att, L0_gnn_conv_bias, L0_gnn_bn_gamma, L0_gnn_bn_beta, L1_gnn_w1, L1_gnn_b1, L1_gnn_w2, L1_gnn_b2):
    import jax
    import jax.numpy as jnp

    def _L0_gnn_ref(patch_embs, edge_index, edge_attr, Wl, bl, Wr, br, att, conv_bias, bn_gamma, bn_beta):
        import jax, jax.numpy as jnp
        import numpy as np
        N = 3125
        E = 50000
        H = 8
        C = 32
        L = 3
        NEG_SLOPE = 0.2
        BN_EPS = 1e-05

        def gatv2_layer(x, Wl, bl, Wr, br, att, bias, src, dst, n):
            xl = (x @ Wl + bl).reshape(n, H, C)
            xr = (x @ Wr + br).reshape(n, H, C)
            e = jax.nn.leaky_relu(xl[src] + xr[dst], NEG_SLOPE)
            logits = jnp.einsum('ehc,hc->eh', e, att)
            m = jax.ops.segment_max(logits, dst, num_segments=n)
            m = jnp.where(jnp.isfinite(m), m, 0.0)
            p = jnp.exp(logits - jax.lax.stop_gradient(m)[dst])
            denom = jax.ops.segment_sum(p, dst, num_segments=n)
            alpha = p / (denom[dst] + 1e-16)
            out = jax.ops.segment_sum(xl[src] * alpha[:, :, None], dst, num_segments=n)
            return out.mean(axis=1) + bias

        def batchnorm_train(x, gamma, beta):
            mu = x.mean(axis=0)
            var = x.var(axis=0)
            return (x - mu) * jax.lax.rsqrt(var + BN_EPS) * gamma + beta
        n = patch_embs.shape[0]
        loops = jnp.arange(n, dtype=edge_index.dtype)
        src = jnp.concatenate([edge_index[0], loops])
        dst = jnp.concatenate([edge_index[1], loops])
        x = patch_embs
        h1 = gatv2_layer(x, Wl[0], bl[0], Wr[0], br[0], att[0], conv_bias[0], src, dst, n)
        x = batchnorm_train(jax.nn.leaky_relu(h1, 0.01) + x, bn_gamma[0], bn_beta[0])
        h2 = gatv2_layer(x, Wl[1], bl[1], Wr[1], br[1], att[1], conv_bias[1], src, dst, n)
        x = batchnorm_train(jax.nn.leaky_relu(h2, 0.01) + x, bn_gamma[1], bn_beta[1])
        h3 = gatv2_layer(x, Wl[2], bl[2], Wr[2], br[2], att[2], conv_bias[2], src, dst, n)
        x = batchnorm_train(h3 + x, bn_gamma[2], bn_beta[2])
        return x

    def _L1_gnn_ref(features, abs_distances, rel_vec, edge_index, w1, b1, w2, b2):
        import jax, jax.numpy as jnp
        import numpy as np
        from math import factorial, pi, sqrt
        MUL = 8
        RS = [(MUL, 0), (MUL, 1)]
        N_NODES = 1250
        N_EDGES = 40000
        FEAT_DIM = sum((m * (2 * l + 1) for m, l in RS))
        R_DIM = sum((mo * mi * (2 * min(lo, li) + 1) for mo, lo in RS for mi, li in RS))
        HIDDEN = 64

        def _cg(j1, j2, j3, m1, m2, m3):
            if m1 + m2 != m3:
                return 0.0
            f = factorial
            pre = sqrt((2 * j3 + 1) * f(j3 + j1 - j2) * f(j3 - j1 + j2) * f(j1 + j2 - j3) / f(j1 + j2 + j3 + 1))
            pre *= sqrt(f(j3 + m3) * f(j3 - m3) * f(j1 - m1) * f(j1 + m1) * f(j2 - m2) * f(j2 + m2))
            kmin = max(0, j2 - j3 - m1, j1 - j3 + m2)
            kmax = min(j1 + j2 - j3, j1 - m1, j2 + m2)
            s = 0.0
            for k in range(kmin, kmax + 1):
                s += (-1) ** k / (f(k) * f(j1 + j2 - j3 - k) * f(j1 - m1 - k) * f(j2 + m2 - k) * f(j3 - j2 + m1 + k) * f(j3 - j1 - m2 + k))
            return pre * s

        def _w3j_complex(l1, l2, l3):
            w = np.zeros((2 * l1 + 1, 2 * l2 + 1, 2 * l3 + 1))
            for m1 in range(-l1, l1 + 1):
                for m2 in range(-l2, l2 + 1):
                    m3 = -(m1 + m2)
                    if abs(m3) <= l3:
                        w[m1 + l1, m2 + l2, m3 + l3] = (-1) ** (l1 - l2 - m3) / sqrt(2 * l3 + 1) * _cg(l1, l2, l3, m1, m2, -m3)
            return w

        def _A(l):
            A = np.zeros((2 * l + 1, 2 * l + 1), dtype=complex)
            A[l, l] = 1.0
            for m in range(1, l + 1):
                A[l + m, l + m] = (-1) ** m / sqrt(2)
                A[l + m, l - m] = 1.0 / sqrt(2)
                A[l - m, l - m] = 1j / sqrt(2)
                A[l - m, l + m] = -1j * (-1) ** m / sqrt(2)
            return A

        def real_w3j(l1, l2, l3):
            wc = _w3j_complex(l1, l2, l3).astype(complex)
            wr = np.einsum('abc,ma,nb,oc->mno', wc, _A(l1).conj(), _A(l2).conj(), _A(l3).conj())
            i = int(np.argmax(np.abs(wr)))
            ph = wr.flat[i] / abs(wr.flat[i])
            wr = wr / ph
            assert np.abs(wr.imag).max() < 1e-10
            return np.real(wr).astype(np.float32)
        _W3J = {}
        for _mo, _lo in RS:
            for _mi, _li in RS:
                for _lf in range(abs(_lo - _li), _lo + _li + 1):
                    if (_lo, _lf, _li) not in _W3J:
                        _W3J[_lo, _lf, _li] = jnp.asarray(real_w3j(_lo, _lf, _li))
        _NORM = []
        for _mo, _lo in RS:
            _num = sum((mi * (2 * min(_lo, li) + 1) for mi, li in RS))
            _NORM.append(sqrt(4.0 * pi) * sqrt(2.0 * _lo + 1.0) / sqrt(_num))
        _F_OFFS = [0] + list(np.cumsum([mi * (2 * li + 1) for mi, li in RS]))

        def spherical_harmonics(rel_vec):
            r = rel_vec / jnp.linalg.norm(rel_vec, axis=-1, keepdims=True)
            x, y, z = (r[:, 0], r[:, 1], r[:, 2])
            y0 = jnp.full_like(x, 0.5 / sqrt(pi))[:, None]
            c1 = sqrt(3.0 / (4.0 * pi))
            y1 = c1 * jnp.stack([y, z, x], axis=-1)
            c2a = 0.5 * sqrt(15.0 / pi)
            c2b = 0.25 * sqrt(5.0 / pi)
            c2c = 0.25 * sqrt(15.0 / pi)
            y2 = jnp.stack([c2a * x * y, c2a * y * z, c2b * (3.0 * z * z - 1.0), c2a * x * z, c2c * (x * x - y * y)], axis=-1)
            return jnp.concatenate([y0, y1, y2], axis=-1)
        src, dst = (edge_index[0], edge_index[1])
        R = jax.nn.relu(abs_distances[:, None] @ w1 + b1) @ w2 + b2
        Y = spherical_harmonics(rel_vec)
        Fj = features[src]
        E = Fj.shape[0]
        msg_blocks = []
        r_off = 0
        for i, (mo, lo) in enumerate(RS):
            acc = jnp.zeros((E, mo, 2 * lo + 1), dtype=features.dtype)
            for j, (mi, li) in enumerate(RS):
                n_lf = 2 * min(lo, li) + 1
                sz = mo * mi * n_lf
                Rb = R[:, r_off:r_off + sz].reshape(E, mo, mi, n_lf)
                r_off += sz
                Fb = Fj[:, _F_OFFS[j]:_F_OFFS[j + 1]].reshape(E, mi, 2 * li + 1)
                for k, lf in enumerate(range(abs(lo - li), lo + li + 1)):
                    C = _W3J[lo, lf, li]
                    Yf = Y[:, lf * lf:(lf + 1) * (lf + 1)]
                    acc = acc + _NORM[i] * jnp.einsum('euv,ef,evi,ofi->euo', Rb[..., k], Yf, Fb, C)
            msg_blocks.append(acc.reshape(E, -1))
        msg = jnp.concatenate(msg_blocks, axis=-1)
        out = jnp.zeros((features.shape[0], msg.shape[1]), dtype=features.dtype)
        out = out.at[dst].add(msg)
        return out
    edge_index = jnp.stack([src, dst])
    x = _layernorm(x + _L0_gnn_ref(x, edge_index, edge_weight1, L0_gnn_Wl, L0_gnn_bl, L0_gnn_Wr, L0_gnn_br, L0_gnn_att, L0_gnn_conv_bias, L0_gnn_bn_gamma, L0_gnn_bn_beta), axis=-1)
    x = _layernorm(x + _L1_gnn_ref(x, edge_weight, edge_attr_3, edge_index, L1_gnn_w1, L1_gnn_b1, L1_gnn_w2, L1_gnn_b2), axis=-1)
    return x

_drawn_inputs = setup_inputs


def setup_inputs(seed=0):
    import zlib

    import numpy as np

    out = dict(_drawn_inputs(seed))
    spreads = {'L0_gnn_bl': (0.0, 0.76),
     'L0_gnn_br': (0.0, 0.8),
     'L0_gnn_conv_bias': (0.0, 0.312),
     'L0_gnn_bn_gamma': (1.0, 0.2),
     'L0_gnn_bn_beta': (0.0, 0.1),
     'L1_gnn_b1': (0.0, 0.1),
     'L1_gnn_b2': (0.0, 0.1)}
    factors = {}
    for name, (base, spread) in spreads.items():
        noise = np.random.default_rng([zlib.crc32(name.encode()), seed]).standard_normal(out[name].shape)
        drawn = base * np.exp(spread * noise) if base else spread * noise
        out[name] = jnp.asarray(drawn.astype(out[name].dtype))
    for name, factor in factors.items():
        out[name] = (out[name] * factor).astype(out[name].dtype)
    return out
```

```python
from contextlib import ExitStack
from math import pi, sqrt

import concourse.bass as bass
import numpy as np
from concourse import mybir

P = 128
N, C, H, LAYERS, E = 6250, 32, 8, 3, 106250
BLOCKS = -(-N // P)
NB = 4 * -(-BLOCKS // 4)
PAIR = 2 * P
PAIRS = -(-E // PAIR)
ROWS = PAIRS + 1
S6 = 6
BODIES = 8
GS = S6 * BODIES
GROUPS = -(-(PAIRS + BLOCKS - 1) // GS)
NS = GROUPS * GS
NSP = -(-NS // P) * P
KQ = NSP // P
J = 3
CH = 16
CW = J * PAIR
C1 = C + 1
HC = H * C
AGG = H * C1 + H
ZW = HC + H
BIG = 1.0e30
NOWHERE = 8192
NSLOPE = 0.2
EPS = 1e-5
SELF = NB // 2
ZS = SELF + NS
QS = NS // J + SELF
AGGS = NS + GROUPS + 1
AHEAD = 8

ALU = mybir.AluOpType
ACT = mybir.ActivationFunctionType
AX = mybir.AxisListType
F32, BF16, I32 = mybir.dt.float32, mybir.dt.bfloat16, mybir.dt.int32


def steps_of(l, g, i, s):
    return ((l * GROUPS + g) * BODIES + i) * S6 + s


def gatv2_program(nc, x, src, dst, edge_w, edge_v, Wl, bl, Wr, br, att, conv_bias, gamma, beta,
                  w1, b1, w2, b2, out):
    ctx = ExitStack()
    with ctx:
        def sb(name, shape, dt=F32):
            return ctx.enter_context(nc.sbuf_tensor(name, shape, dt))

        def sem(name):
            return ctx.enter_context(nc.semaphore(name))

        def dram(name, shape, dt=F32):
            return nc.dram_tensor(name, shape, dt, kind="Internal").ap()

        table = dram("table", (P * BLOCKS, C))
        keys = dram("keys", (1, NSP * PAIR + 2))
        dlocs = dram("dlocs", (1, NSP * PAIR), BF16)
        flags = dram("flags", (P, GROUPS, 3 * CW + 1), BF16)
        w_rows = dram("w_rows", (1, NSP * PAIR))
        v_edges = dram("v_edges", (P, NSP * 2 * 3))

        xn = sb("xn", [P, NB, C])
        hn = sb("hn", [P, NB, C])
        x3 = sb("x3", [P, NB, 3 * C], BF16)
        acc = sb("acc", [P, NB, AGG])
        self_l = sb("self_l", [P, NB, H])
        brow = sb("brow", [1, NSP], I32)
        srci = sb("srci", [P, NSP, 2], I32)
        ndloc = sb("ndloc", [P, NSP, 2])
        laste = sb("laste", [P, NSP, 2])
        ident = sb("ident", [P, P])
        iota_f = sb("iota_f", [P, P])
        iota_p = sb("iota_p", [P, 1])
        mask_c = sb("mask_c", [P, CH])
        sel_h = sb("sel_h", [P, H])
        sel_ht = sb("sel_ht", [H, P])
        ones = sb("ones", [P, P])
        ones_b = sb("ones_b", [96, P], BF16)
        wz = sb("wz", [P, LAYERS, ZW])
        bz = sb("bz", [96, LAYERS, ZW], BF16)
        atts = sb("atts", [P, LAYERS, HC])
        wn = sb("wn", [99, LAYERS, 3, C])
        cb = sb("cb", [P, LAYERS, C])
        gm = sb("gm", [P, LAYERS, C])
        bt = sb("bt", [P, LAYERS, C])
        idx = sb("idx", [P, S6, 2], I32)
        xg = sb("xg", [P, S6, 2, P])
        xs = sb("xs", [P, 2, GS, 2, C1])
        dr = sb("dr", [P, S6, PAIR], BF16)
        oht = sb("oht", [P, 2, PAIR], BF16)
        xt = sb("xt", [P, 2, PAIR])
        dist = sb("dist", [P, 2, P])
        u = sb("u", [P, 2, 2, HC])
        lr = sb("lr", [P, 2, J, 2, H])
        lin = sb("lin", [P, 2, J, 2, H])
        oh = sb("oh", [P, 2, 2, P])
        px = sb("px", [P, 2, 2, AGG])
        lg = sb("lg", [P, J * 2, CH, H])
        pg = sb("pg", [P, J * 2, CH, H])
        mg = sb("mg", [P, J * 2, CH, H])
        fl = sb("fl", [P, 3 * CW + 1], BF16)
        run_f = sb("run_f", [P, CW])
        run_b = sb("run_b", [P, CW])
        ends = sb("ends", [P, 4, CH])
        chain = sb("chain", [H, 4, CH])
        carry = sb("carry", [H, 2, CH + 1])
        back = sb("back", [P, 2, CH])
        carried = sb("carried", [P, 2])
        fix = sb("fix", [H, 4])
        fixd = sb("fixd", [H, H])
        first = sb("first", [H, GROUPS])
        firstb = sb("firstb", [H, GROUPS], BF16)
        fixn = sb("fixn", [P, H])
        zero1 = sb("zero1", [1, 2])
        fhot = sb("fhot", [H, P])
        xw = sb("xw", [P, 2, 2, P])
        gate = sb("gate", [P, 4, NB, H])
        gb = sb("gb", [P, 2, 2, H * C1])
        xp = sb("xp", [P, 2, 2, HC])
        at = sb("at", [99, 2, 2, 3 * P])
        slope = sb("slope", [P, LAYERS])
        real = sb("real", [P, NB])
        hsum = sb("hsum", [P, 4, C])

        psum = ctx.enter_context(nc.psum_tensor("psum", [P, 8, 512], F32))

        def z_ps(r, lo=0, hi=ZW):
            return psum[:, 2 * r:2 * r + 2, lo:hi]

        def xt_ps(r):
            return psum[:, 4 + r, :]

        def agg_ps(r):
            return psum[:, 6 + r, 0:AGG]

        lt_ps = psum[:, 0:2, :].rearrange("p a b -> p (a b)")[:, 0:CW]
        tp_ps = psum[:, 2:4, :].rearrange("p a b -> p (a b)")[:, 0:CW]

        def carver(flat):
            at = [0]

            def carve(shape, dt=F32, parts=P):
                n = int(np.prod(shape))
                a = flat[0:parts, at[0]:at[0] + (n if dt != BF16 else n // 2)]
                at[0] += n if dt != BF16 else n // 2
                assert at[0] <= flat.shape[1], at
                a = a if dt == F32 else a.bitcast(dt)
                if len(shape) == 1:
                    return a
                names = "abcd"[:len(shape)]
                return a.rearrange(f"p ({' '.join(names)}) -> p {' '.join(names)}", **dict(zip(names, shape)))
            return carve

        in_acc = carver(acc[:].rearrange("p a b -> p (a b)"))
        in_xs = carver(xs[:].rearrange("p a b c d -> p (a b c d)"))
        LANE = ROWS * PAIR // P
        dsti = in_acc([LANE], I32)
        dstf = in_acc([LANE])
        below = in_acc([LANE])
        cnt = in_acc([NB])
        rowf = in_acc([12, NB], parts=1)
        rowi = in_acc([4, NB], I32, parts=1)
        col = in_acc([2], parts=BLOCKS - 1)
        rd = in_acc([2], parts=BLOCKS - 1)
        mask = in_acc([NSP], parts=BLOCKS - 1)
        iota_k = in_acc([NSP])
        kcol = in_acc([KQ])
        bcol = in_acc([KQ])
        tcol = in_acc([KQ])
        tci = in_acc([KQ], I32)
        iota_i = in_acc([P], I32)
        part_i = in_acc([2], I32)
        part_f = in_acc([2])
        wrow = in_acc([KQ, PAIR])
        vrow = in_acc([KQ, 3 * PAIR])
        vedge = in_acc([NSP, 2, 3])
        watt = in_xs([LAYERS * HC])
        wlin = in_xs([LAYERS * H])
        wtmp = in_xs([LAYERS * HC])
        bsum = in_xs([LAYERS * ZW])
        bsum2 = in_xs([LAYERS * ZW])
        bhb = in_xs([LAYERS * ZW], BF16)
        srow = in_acc([KQ, PAIR], I32)
        drow = in_acc([KQ, PAIR], I32)
        dl = in_xs([KQ, PAIR])
        srcf = in_xs([KQ, PAIR])
        key = u[:].rearrange("p a b c -> p (a b) c")
        kw = sb("kw", [P, KQ, PAIR + 2])
        dlb = sb("dlb", [P, KQ, PAIR], BF16)
        valid = gb[:].rearrange("p a b c -> p (a b c)")[:, 0:KQ * PAIR].rearrange("p (q e) -> p q e", q=KQ)
        lastr = px[:].rearrange("p a b c -> p (a b c)")[:, 0:KQ * PAIR].rearrange("p (q e) -> p q e", q=KQ)
        in_l1 = carver(acc[:].rearrange("p a b -> p (a b)"))
        OPS = 12
        START = 64
        vec = in_l1([NSP, 2, 3])
        unit = in_l1([NS, 2, 3])
        norm = in_l1([2, NS, 2])
        acc1 = in_l1([NB, C])
        wb = in_l1([S6, PAIR], parts=64)
        rb = in_l1([2, 2, P])
        gk = in_l1([2, 6, 3, 4])
        ta = in_l1([2, 2, 16])
        xo = in_l1([2, 2, 4, 16])
        gp = in_l1([2, 2, 8, 12])
        mg1 = in_l1([2, 2, 24])
        msg = in_l1([2, 2, C])
        stat = in_l1([4, NB])
        sprod = xp[:, :, :, 0:24]
        pa = u[:]
        hid = xt
        w2e = sb("w2e", [65, 384])
        pb = xs[:].rearrange("p a b c d -> p (a b c d)")[:, 0:4 * 384].rearrange("p (a b c) -> p a b c", a=2, b=2)
        w2raw = xs[:].rearrange("p a b c d -> p (a b c d)")[0:65, 2048:2048 + 384]
        w1c = sb("w1c", [64, 2])
        kwins = [t[:].rearrange("p a b c -> p (a b c)")[:, 0:CW + 2] for t in (xp, u)]

        s_in = sem("s_in")
        s_wt = sem("s_wt")
        s_iota = sem("s_iota")
        s_set = sem("s_set")
        s_pe = sem("s_pe")
        s_rows = sem("s_rows")
        s_rows2 = sem("s_rows2")
        s_seq = sem("s_seq")
        s_kw = sem("s_kw")
        s_tr = sem("s_tr")
        s_trc = sem("s_trc")
        s_win = [sem(f"s_win{k}") for k in range(2)]
        s_flag = sem("s_flag")
        s_flst = sem("s_flst")
        s_ready = sem("s_ready")
        gat = [sem(f"gat{s}") for s in range(S6)]
        drl = [sem(f"drl{h}") for h in range(2)]
        front_done = sem("front_done")
        xt_done = sem("xt_done")
        xs_done = sem("xs_done")
        z_done = sem("z_done")
        u_done = sem("u_done")
        r_done = sem("r_done")
        lin_done = sem("lin_done")
        l_done = sem("l_done")
        oht_done = sem("oht_done")
        abs_done = sem("abs_done")
        relu_done = sem("relu_done")
        px_done = sem("px_done")
        pm_done = sem("pm_done")
        agg_done = sem("agg_done")
        acc_done = sem("acc_done")
        idx_done = sem("idx_done")
        xw_done = sem("xw_done")
        fl_done = sem("fl_done")
        c_lt = sem("c_lt")
        c_ends = sem("c_ends")
        c_ch = sem("c_ch")
        c_car = sem("c_car")
        c_bk = sem("c_bk")
        c_t = sem("c_t")
        c_fx = sem("c_fx")
        c_fe = sem("c_fe")
        c_fd = sem("c_fd")
        c_fn = sem("c_fn")
        c_tp = sem("c_tp")
        c_sub = sem("c_sub")
        c_pg = sem("c_pg")
        c_end = sem("c_end")
        x_new = sem("x_new")
        x3_new = sem("x3_new")
        tab_new = sem("tab_new")
        f_exp = sem("f_exp")
        f_gate = sem("f_gate")
        f_g = sem("f_g")
        xp_done = sem("xp_done")
        gb_done = sem("gb_done")
        gt_done = sem("gt_done")
        at_done = sem("at_done")
        o_done = sem("o_done")
        h_done = sem("h_done")
        n_sum = sem("n_sum")
        n_all = sem("n_all")
        n_var = sem("n_var")
        n_sqrt = sem("n_sqrt")

        x0_in = sem("x0_in")
        v_in = sem("v_in")
        ln_var = sem("ln_var")
        ln_sqrt = sem("ln_sqrt")
        l1_go = sem("l1_go")
        wbl = [sem(f"wbl{h}") for h in range(2)]
        hid_done = sem("hid_done")
        rr_done = sem("rr_done")
        rb_done = sem("rb_done")
        ta_done = sem("ta_done")
        gk_done = sem("gk_done")
        pb_done = sem("pb_done")
        mix_done = sem("mix_done")
        oh1_done = sem("oh1_done")
        abs1_done = sem("abs1_done")
        ag1_done = sem("ag1_done")
        passed = sem("passed")
        s_out = sem("s_out")

        block = ctx.enter_context(nc.Block())
        flat_w = w_rows.rearrange("o (q p e) -> p (o q) e", q=KQ, p=P)
        flat_k = keys[:, 1:1 + NSP * PAIR].rearrange("o (q p e) -> p (o q) e", q=KQ, p=P)
        flat_d = dlocs.rearrange("o (q p e) -> p (o q) e", q=KQ, p=P)

        WEIGHT_LOADS = 26
        COUNTS, BOUNDS, MASKS, STEPS, SEQUENCES, FIELDS = range(1, 7)

        @block.sync
        def _(sp):
            sp.dma_start(dsti, dst.rearrange("r e -> (r e)").rearrange("(p e) -> p e", p=P)).then_inc(s_in, 16)
            sp.dma_start(xn[:, 0:BLOCKS, :], x).then_inc(s_in, 16)
            for k in range(3):
                sp.dma_start(wz[32 * k:32 * k + 32, :, 0:HC], Wr.rearrange("l c k -> c l k")).then_inc(s_wt, 16)
            sp.dma_start(wz[96:128, :, 0:HC], Wl.rearrange("l c k -> c l k")).then_inc(s_wt, 16)
            sp.dma_start(watt, att.rearrange("l h c -> (l h c)").partition_broadcast(P)).then_inc(s_wt, 16)
            sp.dma_start(bsum.rearrange("p (l z) -> p l z", l=LAYERS)[0:96, :, 0:HC], bl.partition_broadcast(96)).then_inc(s_wt, 16)
            sp.dma_start(bsum2.rearrange("p (l z) -> p l z", l=LAYERS)[0:96, :, 0:HC], br.partition_broadcast(96)).then_inc(s_wt, 16)
            for t, w in ((cb, conv_bias), (gm, gamma), (bt, beta)):
                sp.dma_start(t[:], w.partition_broadcast(P)).then_inc(s_wt, 16)
            for h in range(H):
                r = (h % 3) * C1
                sp.dma_start(wn[r:r + C, :, h // 3, :],
                             Wl[:, :, h * C:(h + 1) * C].rearrange("l c k -> c l k")).then_inc(s_wt, 16)
                sp.dma_start(wn[r + C:r + C1, :, h // 3, :],
                             bl[:, h * C:(h + 1) * C].rearrange("(o l) k -> o l k", o=1)).then_inc(s_wt, 16)
            sp.wait_ge(s_rows2, 16 * 2 * KQ)
            sp.dma_start(flat_w, wrow).then_inc(s_seq, 16)
            sp.wait_ge(s_set, SEQUENCES)
            sp.dma_start(flat_k, key).then_inc(s_seq, 16)
            sp.dma_start(flat_d, dlb[:]).then_inc(s_seq, 16)
            sp.dma_start(keys[:, 0:1], zero1[:, 0:1]).then_inc(s_seq, 16)
            sp.dma_start(keys[:, NSP * PAIR + 1:NSP * PAIR + 2], zero1[:, 1:2]).then_inc(s_seq, 16)
            sp.wait_ge(s_seq, 80)
            for q in range(KQ):
                sp.dma_start(kw[:, q, :], bass.AP(tensor=keys.tensor, offset=q * P * PAIR,
                                                  ap=[[PAIR, P], [1, PAIR + 2]])).then_inc(s_kw, 16)
            sp.dma_start(firstb[:], bass.AP(tensor=dlocs.tensor, offset=0,
                                            ap=[[0, H], [GS * PAIR, GROUPS]]),
                         allow_slow_non_contiguous=True).then_inc(s_kw, 16)
            for g in range(GROUPS + 2):
                if g >= 2:
                    sp.wait_ge(s_flag, 2 * (g - 2) + 2)
                    sp.dma_start(flags[:, g - 2, :], fl[:]).then_inc(s_flst, 16)
                if g < GROUPS:
                    sp.dma_start(kwins[g % 2], bass.AP(tensor=keys.tensor, offset=g * GS * PAIR,
                                                       ap=[[CW, CH], [0, H], [1, CW + 2]])).then_inc(s_win[g % 2], 16)
            sp.wait_ge(s_ready, 1)
            sp.dma_start(v_edges, vedge.rearrange("p k u f -> p (k u f)")).then_inc(s_seq, 16)
            sp.wait_ge(s_seq, 96)
            sp.wait_ge(s_flst, 16 * GROUPS)

            def load_places(l, g, i):
                for half in range(2):
                    n = steps_of(l, g, i, 3 * half)
                    k0 = (g * BODIES + i) * S6 + 3 * half
                    sp.wait_ge(oht_done, AHEAD + n - 3)
                    sp.dma_start(dr[:, 3 * half:3 * half + 3, :].rearrange("p s e -> p (s e)"),
                                 dlocs[0, bass.ds(k0 * PAIR, 3 * PAIR)].partition_broadcast(P)).then_inc(drl[half], 16)

            with sp.Fori(0, LAYERS) as l:
                sp.wait_ge(x_new, l + 1)
                sp.dma_start(table.rearrange("(p b) c -> p b c", p=P), xn[:, 0:BLOCKS, :]).then_inc(tab_new, 16)
                with sp.Fori(0, GROUPS) as g:
                    with sp.Fori(0, BODIES) as i:
                        load_places(l, g, i)
                    sp.wait_ge(c_end, l * GROUPS + g + 1)
                    sp.dma_start(fl[:], flags[:, bass.ds(g, 1), :].rearrange("p o w -> p (o w)")).then_inc(fl_done, 16)

            sp.wait_ge(x_new, LAYERS + 1)
            sp.dma_start(hn[:, 0:BLOCKS, :], x).then_inc(x0_in, 16)
            sp.dma_start(vec.rearrange("p k e f -> p (k e f)"), v_edges).then_inc(v_in, 16)
            sp.dma_start(w2raw[0:64], w2).then_inc(v_in, 16)
            sp.dma_start(w2raw[64:65], b2.rearrange("(o k) -> o k", o=1)).then_inc(v_in, 16)
            sp.dma_start(w1c[:, 0:1], w1.rearrange("o q -> q o")).then_inc(v_in, 16)
            sp.dma_start(w1c[:, 1:2], b1.rearrange("(q o) -> q o", o=1)).then_inc(v_in, 16)
            sp.wait_ge(x_new, LAYERS + 2)
            sp.dma_start(table.rearrange("(p b) c -> p b c", p=P), xn[:, 0:BLOCKS, :]).then_inc(tab_new, 16)
            with sp.Fori(0, NS // S6) as i:
                for half in range(2):
                    k0 = i * S6 + 3 * half
                    sp.wait_ge(hid_done, AHEAD + k0 - 3)
                    sp.dma_start(wb[:, 3 * half:3 * half + 3, :].rearrange("p s e -> p (s e)"),
                                 w_rows[0, bass.ds(k0 * PAIR, 3 * PAIR)].partition_broadcast(64)).then_inc(wbl[half], 16)
            sp.wait_ge(x_new, LAYERS + 3)
            sp.dma_start(out, xn[:, 0:BLOCKS, :]).then_inc(s_out, 16)
            sp.wait_ge(s_out, 16)

        @block.gpsimd
        def _(pool):
            io = dict(allow_small_or_imprecise_dtypes=True)
            nc.gpsimd.iota(iota_f[:], pattern=[[1, P]], base=0, channel_multiplier=0, **io).then_inc(s_iota, 1)
            nc.gpsimd.iota(iota_p[:], pattern=[[1, 1]], base=0, channel_multiplier=1, **io).then_inc(s_iota, 1)
            nc.gpsimd.iota(iota_k, pattern=[[1, NSP]], base=0, channel_multiplier=0, **io).then_inc(s_iota, 1)
            nc.gpsimd.iota(kcol, pattern=[[P, KQ]], base=0, channel_multiplier=1, **io).then_inc(s_iota, 1)
            nc.gpsimd.iota(iota_i, pattern=[[1, P]], base=0, channel_multiplier=0).then_inc(s_iota, 1)
            nc.gpsimd.iota(part_i[:, 0:1], pattern=[[1, 1]], base=0, channel_multiplier=1).then_inc(s_iota, 1)
            nc.gpsimd.memset(xg[:], 0.0)
            pool.wait_ge(s_set, STEPS)
            for table_rows, to, done in ((src, srow, s_rows), (dst, drow, s_rows), (edge_w, wrow, s_rows2), (edge_v, vrow, s_rows2)):
                for q in range(KQ):
                    nc.gpsimd.indirect_dma_start(
                        out=to[:, q, :], out_offset=None, in_=table_rows,
                        in_offset=bass.IndirectOffsetOnAxis(ap=tci[:, q:q + 1], axis=0)).then_inc(done, 16)

            def then():
                pool.sem_inc(passed, 1)

            pool.sem_inc(idx_done, AHEAD)
            pool.sem_inc(xp_done, AHEAD)
            pool.wait_ge(s_seq, 96)
            pool.wait_ge(s_ready, 1)
            with pool.Fori(0, LAYERS) as l:
                pool.wait_ge(x_new, l + 1)
                then()
                nc.gpsimd.memset(acc[:], 0.0).then_inc(acc_done, 1)
                pool.wait_ge(tab_new, 16 * (l + 1))
                then()
                with pool.Fori(0, GROUPS) as g:
                    with pool.Fori(0, BODIES) as i:
                        body = (l * GROUPS + g) * BODIES + i
                        k0 = (g * BODIES + i) * S6
                        for half in range(2):
                            a = 3 * half
                            pool.wait_ge(front_done, AHEAD + l * ZS + k0 + a + 3 - S6)
                            nc.gpsimd.tensor_copy(idx[:, a:a + 3, :], srci[:, bass.ds(k0 + a, 3), :]).then_inc(idx_done, 1)
                            pool.wait_ge(idx_done, AHEAD + 2 * body + half + 1)
                            for s in range(a, a + 3):
                                pool.wait_ge(front_done, AHEAD + l * ZS + k0 + s + 1 - S6)
                                pool.wait_ge(xs_done, AHEAD + l * NS + k0 + s + 1 - S6)
                                then()
                                for t in range(2):
                                    nc.gpsimd.indirect_dma_start(
                                        out=xg[:, s, t, 96:128], out_offset=None, in_=table,
                                        in_offset=bass.IndirectOffsetOnAxis(ap=idx[:, s, t:t + 1], axis=0)).then_inc(gat[s], 16)
                pool.wait_ge(f_g, l + 1)
                then()
                with pool.Fori(0, SELF // 2) as i:
                    for r in range(2):
                        m = l * SELF + i * 2 + r
                        pool.wait_ge(gb_done, AHEAD + m - 1)
                        nc.gpsimd.tensor_tensor(
                            xp[:, r].rearrange("p b (h c) -> p b h c", h=H),
                            xn[:, bass.ds(i * 4 + 2 * r, 2), :].unsqueeze(2).to_broadcast([P, 2, H, C]),
                            gate[:, 3, bass.ds(i * 4 + 2 * r, 2), :].unsqueeze(3).to_broadcast([P, 2, H, C]),
                            ALU.mult).then_inc(xp_done, 1)

            def gather1(k, s):
                pool.wait_ge(ta_done, AHEAD + k + 1 - S6)
                pool.wait_ge(mix_done, START + (k - S6 + 1) * OPS)
                pool.wait_ge(pb_done, AHEAD + k + 1 - S6)
                then()
                for e in range(2):
                    nc.gpsimd.indirect_dma_start(
                        out=xg[:, s, e, 96:128], out_offset=None, in_=table,
                        in_offset=bass.IndirectOffsetOnAxis(ap=idx[:, s, e:e + 1], axis=0)).then_inc(gat[s], 16)

            def numbers1(k, half):
                pool.wait_ge(ta_done, AHEAD + k + 3 - S6)
                nc.gpsimd.tensor_copy(idx[:, 3 * half:3 * half + 3, :], srci[:, bass.ds(k, 3), :]).then_inc(idx_done, 1)
                pool.wait_ge(idx_done, AHEAD + LAYERS * GROUPS * BODIES * 2 + k // 3 + 1)

            def product(k, s):
                r = s % 2
                pool.wait_ge(rb_done, AHEAD + k + 1)
                pool.wait_ge(mix_done, START + (k - 2) * OPS + 6)
                pool.wait_ge(gat[s], 32 * (LAYERS * GROUPS * BODIES) + 32 * (k // S6) + 32)
                for e, n in ((0, 3), (1, 2)):
                    last = nc.gpsimd.tensor_tensor(
                        pb[:, r, e].rearrange("p (i u v) -> p i u v", i=3, v=8)[:, 0:n],
                        rb[:, r, e].rearrange("p (u v) -> p u v", v=8).unsqueeze(1).to_broadcast([P, n, 16, 8]),
                        xg[:, s, e, 104:128].rearrange("p (v i) -> p i v", i=3)[:, 0:n].unsqueeze(2).to_broadcast([P, n, 16, 8]),
                        ALU.mult)
                last.then_inc(pb_done, 1)

            pool.sem_inc(pb_done, AHEAD)
            pool.wait_ge(tab_new, 16 * (LAYERS + 1))
            numbers1(0, 0)
            for s in range(3):
                gather1(s, s)
            with pool.Fori(0, NS // S6 - 1) as i:
                for s in range(S6):
                    k = i * S6 + s
                    if s % 3 == 0:
                        numbers1(k + 3, (s // 3 + 1) % 2)
                    gather1(k + 3, (s + 3) % S6)
                    product(k, s)
            for s in range(S6):
                k = NS - S6 + s
                if s == 0:
                    numbers1(k + 3, 1)
                if s < 3:
                    gather1(k + 3, s + 3)
                product(k, s)

        @block.tensor
        def _(pe):
            pe.wait_ge(s_set, COUNTS)
            pe.matmul(psum[0:1, 0, 0:NB], ones[:, 0:1], cnt, start=True, stop=True).then_inc(s_pe, 1)
            pe.wait_ge(s_set, BOUNDS)
            pe.matmul(psum[0:BLOCKS - 1, 1, 0:1], rowf[:, 8, 1:BLOCKS], ones[0:1, 0:1], start=True, stop=True)
            pe.matmul(psum[0:BLOCKS - 1, 1, 1:2], rowf[:, 9, 1:BLOCKS], ones[0:1, 0:1], start=True, stop=True).then_inc(s_pe, 1)
            pe.wait_ge(s_set, MASKS)
            for q in range(KQ):
                pe.matmul(psum[:, 2, 2 * q:2 * q + 2], mask[:, q * P:(q + 1) * P], rd, start=True, stop=True)
            pe.matmul(psum[0:1, 3, 0:NSP], rd[:, 0:1], mask, start=True, stop=True).then_inc(s_pe, 1)
            pe.wait_ge(s_set, FIELDS)
            pe.wait_ge(s_rows2, 16 * 2 * KQ)
            for r in range(2 * KQ):
                q, e = r // 2, slice((r % 2) * P, (r % 2) * P + P)
                if r >= 2:
                    pe.wait_ge(s_trc, r - 1)
                for f, rows in enumerate((srcf, dl, lastr)):
                    pe.transpose(psum[:, 4 + 2 * (r % 2), f * P:f * P + P], rows[:, q, e], ident[:])
                for f in range(3):
                    last = pe.transpose(psum[:, 5 + 2 * (r % 2), f * P:f * P + P],
                                        vrow.rearrange("p q (e f) -> p q e f", f=3)[:, q, e, f], ident[:])
                last.then_inc(s_tr, 1)

            pe.sem_inc(front_done, AHEAD)
            pe.sem_inc(z_done, AHEAD)
            pe.sem_inc(agg_done, AHEAD)
            pe.sem_inc(gt_done, AHEAD)
            pe.sem_inc(o_done, AHEAD)

            def front(l, k, s, t):
                r = s % 2
                pe.wait_ge(gat[s], 32 * t + 32)
                pe.wait_ge(xt_done, AHEAD + l * ZS + k - 1)
                for e in range(2):
                    pe.transpose(xt_ps(r)[:, e * P:(e + 1) * P], xg[:, s, e, :], ident[:])
                b = pe.value_load(brow[0:1, bass.ds(k, 1)], min_val=0, max_val=BLOCKS - 1)
                pe.wait_ge(oht_done, AHEAD + l * NS + k + 1)
                pe.matmul(xt_ps(r)[0:96, 0:PAIR], x3[:, bass.ds(b, 1), :].rearrange("p o c -> p (o c)"),
                          oht[:, r, :], start=True, stop=True).then_inc(front_done, 1)

            def zed(l, n, r):
                pe.wait_ge(xt_done, AHEAD + l * ZS + n + 1)
                pe.wait_ge(lin_done, AHEAD + l * ZS + n - 1)
                for e in range(2):
                    out_z = z_ps(r)[:, e, :]
                    pe.matmul(out_z, xt[:, r, e * P:(e + 1) * P], wz[:, bass.ds(l, 1), :].rearrange("p o z -> p (o z)"),
                              start=True, stop=False)
                    last = pe.matmul(out_z, ones_b[:], bz[:, bass.ds(l, 1), :].rearrange("p o z -> p (o z)"),
                                     start=False, stop=True)
                last.then_inc(z_done, 1)

            def aggregate(l, g, k, s):
                r = s % 2
                m = l * NS + k
                pe.wait_ge(relu_done, AHEAD + m + 1)
                pe.wait_ge(px_done, AHEAD + m + 1)
                pe.wait_ge(pm_done, AHEAD + m + 1)
                pe.wait_ge(acc_done, AHEAD + l * AGGS + 2 + g + k - 1)
                for e in range(2):
                    last = pe.matmul(agg_ps(r), oh[:, r, e, :], px[:, r, e, :], start=(e == 0), stop=(e == 1))
                last.then_inc(agg_done, 1)

            def pe_body(l, g, i, a, b, ends_group):
                k0 = (g * BODIES + i) * S6
                t = (l * GROUPS + g) * BODIES + i
                for s in range(S6):
                    if a and (s + 2 < S6 or not ends_group):
                        front(l, k0 + s + 2, (s + 2) % S6, t + (s + 2) // S6)
                    if a and (s + 1 < S6 or not ends_group):
                        zed(l, k0 + s + 1, (s + 1) % 2)
                    if b:
                        aggregate(l, g - 1, k0 - GS + s, s)

            def pe_group(l, g, a, b):
                if a:
                    t = (l * GROUPS + g) * BODIES
                    front(l, g * GS, 0, t)
                    front(l, g * GS + 1, 1, t)
                    zed(l, g * GS, 0)
                with pe.Fori(0, BODIES - 1) as i:
                    pe_body(l, g, i, a, b, False)
                pe_body(l, g, BODIES - 1, a, b, True)

            def pe_maxima(l, g):
                q = l * GROUPS + g
                pe.wait_ge(l_done, AHEAD + l * QS + (g + 1) * CH)
                for k in range(2 * J):
                    last = pe.transpose(lt_ps[:, k * P:(k + 1) * P], lg[:, k].rearrange("p c h -> p (c h)"), ident[:])
                last.then_inc(c_lt, 1)
                pe.wait_ge(c_ends, q + 1)
                pe.matmul(psum[0:H, 6, 0:4 * CH], sel_h[:], ends[:].rearrange("p a c -> p (a c)"),
                          start=True, stop=True).then_inc(c_ch, 1)
                pe.wait_ge(c_car, q + 1)
                pe.matmul(psum[:, 7, 0:2 * CH], sel_ht[:], carry[:, :, 0:CH], start=True, stop=True).then_inc(c_bk, 1)
                pe.wait_ge(c_t, q + 1)
                for k in range(2 * J):
                    last = pe.transpose(tp_ps[:, k * P:(k + 1) * P], run_f[:, k * P:(k + 1) * P], ident[:])
                last.then_inc(c_tp, 1)
                pe.wait_ge(c_fd, q + 1)
                pe.matmul(psum[:, 6, 0:H], fhot[:], fixd[:], start=True, stop=True).then_inc(c_fn, 1)

            def self_front(l, m, r):
                pe.wait_ge(xw_done, AHEAD + l * SELF + m + 1)
                pe.wait_ge(xt_done, AHEAD + l * ZS + NS + m - 1)
                for e in range(2):
                    last = pe.transpose(xt_ps(r)[:, e * P:(e + 1) * P], xw[:, r, e, :], ident[:])
                last.then_inc(front_done, 1)

            def transposed_sums(l, m, r):
                pe.wait_ge(gb_done, AHEAD + l * SELF + m + 1)
                pe.wait_ge(at_done, AHEAD + l * SELF + m - 1)
                for e in range(2):
                    for j in range(3):
                        w = min(3, H - 3 * j) * C1
                        last = pe.transpose(psum[0:w, 2 * r + e, j * P:(j + 1) * P],
                                            gb[:, r, e, 99 * j:99 * j + w], ident[:])
                last.then_inc(gt_done, 1)

            def layer_output(l, m, r):
                pe.wait_ge(at_done, AHEAD + l * SELF + m + 1)
                pe.wait_ge(h_done, AHEAD + l * SELF + m - 1)
                for e in range(2):
                    for j in range(3):
                        w = min(3, H - 3 * j) * C1
                        last = pe.matmul(psum[:, 4 + r, e * C:(e + 1) * C], at[0:w, r, e, j * P:(j + 1) * P],
                                         wn[0:w, bass.ds(l, 1), j, :].rearrange("p o c -> p (o c)"),
                                         start=(j == 0), stop=(j == 2))
                last.then_inc(o_done, 1)

            with pe.Fori(0, LAYERS) as l:
                pe.wait_ge(x3_new, l + 1)
                pe_group(l, 0, True, False)
                pe_maxima(l, 0)
                with pe.Fori(1, GROUPS) as g:
                    pe_group(l, g, True, True)
                    pe_maxima(l, g)
                pe_group(l, GROUPS, False, True)
                for r in range(2):
                    self_front(l, r, r)
                with pe.Fori(0, SELF // 2 - 1) as i:
                    for r in range(2):
                        zed(l, NS + i * 2 + r, r)
                    for r in range(2):
                        self_front(l, i * 2 + 2 + r, r)
                for r in range(2):
                    zed(l, NS + SELF - 2 + r, r)
                transposed_sums(l, 0, 0)
                with pe.Fori(0, SELF // 2 - 1) as i:
                    for r in range(2):
                        transposed_sums(l, i * 2 + r + 1, 1 - r)
                        layer_output(l, i * 2 + r, r)
                transposed_sums(l, SELF - 1, 1)
                layer_output(l, SELF - 2, 0)
                layer_output(l, SELF - 1, 1)
                for k in range(2):
                    pe.wait_ge(n_sum, 2 * l + k + 1)
                    pe.matmul(psum[:, 6 + k, 0:C], ones[:], hsum[:, k, :], start=True, stop=True).then_inc(n_all, 1)

            pe.sem_inc(rr_done, AHEAD)
            pe.sem_inc(ag1_done, AHEAD)
            pe.wait_ge(l1_go, 1)

            def radial(k, r):
                pe.wait_ge(hid_done, AHEAD + k + 1)
                pe.wait_ge(rb_done, AHEAD + k - 1)
                pe.wait_ge(mix_done, START + (k - 2) * OPS + 1)
                for e in range(2):
                    rows = hid[0:65, r, e * P:(e + 1) * P]
                    pe.matmul(z_ps(r, 0, HC)[:, e, :], rows, w2e[:, 0:HC], start=True, stop=True)
                    last = pe.matmul(psum[:, 4 + r, e * P:(e + 1) * P], rows, w2e[:, HC:HC + P], start=True, stop=True)
                last.then_inc(rr_done, 1)

            def sum_messages(k, r):
                pe.wait_ge(oh1_done, AHEAD + k + 1)
                pe.wait_ge(mix_done, START + (k + 1) * OPS)
                for e in range(2):
                    last = pe.matmul(psum[:, 6 + r, 0:C], oh[:, r, e, :], msg[:, r, e, :], start=(e == 0), stop=(e == 1))
                last.then_inc(ag1_done, 1)

            radial(0, 0)
            for s in range(S6):
                radial(s + 1, (s + 1) % 2)
                if s > 0:
                    sum_messages(s - 1, 1 - s % 2)
            with pe.Fori(1, NS // S6 - 1) as i:
                for s in range(S6):
                    radial(i * S6 + s + 1, (s + 1) % 2)
                    sum_messages(i * S6 + s - 1, 1 - s % 2)
            for s in range(S6):
                if s + 1 < S6:
                    radial(NS - S6 + s + 1, (s + 1) % 2)
                sum_messages(NS - S6 + s - 1, 1 - s % 2)
            sum_messages(NS - 1, 1)

        @block.scalar
        def _(act):
            op = nc.scalar
            act.sem_inc(xt_done, AHEAD)
            act.sem_inc(lin_done, AHEAD)
            act.sem_inc(xs_done, AHEAD)
            act.sem_inc(pm_done, AHEAD)
            act.sem_inc(abs_done, AHEAD)
            act.sem_inc(relu_done, AHEAD)
            act.sem_inc(xw_done, AHEAD)
            act.sem_inc(at_done, AHEAD)
            act.wait_ge(s_ready, 2)

            def one_hot(l, k, r):
                act.wait_ge(agg_done, AHEAD + l * NS + k - 1)
                act.wait_ge(relu_done, AHEAD + l * NS + k)
                for e in range(2):
                    last = op.activation(dist[:, e, :], iota_f[:], ACT.Abs,
                                         bias=ndloc[:, bass.ds(k, 1), e])
                last.then_inc(abs_done, 1)
                act.wait_ge(abs_done, AHEAD + l * NS + k + 1)
                op.activation(oh[:, r], dist[:], ACT.Relu, bias=1.0, scale=-1.0).then_inc(relu_done, 1)

            def keep(l, g, i, k, s):
                r = s % 2
                act.wait_ge(front_done, AHEAD + l * ZS + k + 1)
                act.wait_ge(z_done, AHEAD + l * ZS + k - 1)
                op.copy(xt[:, r, :], xt_ps(r)[:, 0:PAIR]).then_inc(xt_done, 1)
                op.copy(xs[:, bass.ds((l * GROUPS + g) % 2, 1), bass.ds(i * S6 + s, 1), :, 0:C].rearrange("p o q e c -> p (o q e) c"),
                        xg[:, s % S6, :, 96:128]).then_inc(xs_done, 1)

            def linear(l, n, r, q, c, j):
                if j == 0:
                    act.wait_ge(l_done, AHEAD + l * QS + q - 1)
                act.wait_ge(u_done, AHEAD + l * ZS + n + 1)
                op.copy(lin[:, c, j], z_ps(r, HC, ZW)).then_inc(lin_done, 1)

            def act_body(l, g, i, a, b, ends_group):
                k0 = (g * BODIES + i) * S6
                for s in range(S6):
                    r = s % 2
                    if b:
                        m = l * NS + k0 - GS + s
                        c, j = i * 2 + s // J, s % J
                        one_hot(l, k0 - GS + s, r)
                        op.copy(px[:, r, :, H * C1:AGG],
                                mg[:, 2 * j:2 * j + 2, bass.ds(c, 1), :].rearrange("p e o h -> p e (o h)")).then_inc(pm_done, 1)
                    if a and (s + 2 < S6 or not ends_group):
                        keep(l, g, i, k0 + s + 2, s + 2)
                    if a:
                        linear(l, k0 + s, r, (g * BODIES + i) * 2 + s // J, s // J, s % J)

            def act_group(l, g, a, b):
                if a:
                    keep(l, g, 0, g * GS, 0)
                    keep(l, g, 0, g * GS + 1, 1)
                with act.Fori(0, BODIES - 1) as i:
                    act_body(l, g, i, a, b, False)
                act_body(l, g, BODIES - 1, a, b, True)

            def act_maxima(l, g):
                q = l * GROUPS + g
                act.wait_ge(c_fx, q + 1)
                op.activation(fix[:, 2:3], fix[:, 1:2], ACT.Exp).then_inc(c_fe, 1)
                act.wait_ge(c_sub, q + 1)
                op.activation(pg[:], lg[:], ACT.Exp).then_inc(c_pg, 1)
                act.wait_ge(c_end, q + 2)

            def self_rows(l, m, r):
                act.wait_ge(front_done, AHEAD + l * ZS + NS + m - 1)
                pair = bass.ds(m * 2, 2) if not isinstance(m, int) else slice(m * 2, m * 2 + 2)
                op.copy(xw[:, r, :, 0:C], xn[:, pair, :])
                op.copy(xw[:, r, :, 96:128], xn[:, pair, :]).then_inc(xw_done, 1)

            def self_keep(l, m, r):
                act.wait_ge(front_done, AHEAD + l * ZS + NS + m + 1)
                act.wait_ge(z_done, AHEAD + l * ZS + NS + m - 1)
                op.copy(xt[:, r, :], xt_ps(r)[:, 0:PAIR]).then_inc(xt_done, 1)

            with act.Fori(0, LAYERS) as l:
                act.wait_ge(x_new, l + 1)
                act_group(l, 0, True, False)
                act_maxima(l, 0)
                with act.Fori(1, GROUPS) as g:
                    act_group(l, g, True, True)
                    act_maxima(l, g)
                act_group(l, GROUPS, False, True)
                for r in range(2):
                    self_rows(l, r, r)
                with act.Fori(0, SELF // 2 - 1) as i:
                    for r in range(2):
                        self_keep(l, i * 2 + r, r)
                    for r in range(2):
                        self_rows(l, i * 2 + 2 + r, r)
                    for r in range(2):
                        linear(l, NS + i * 2 + r, r, NS // J + i * 2 + r, r, 0)
                for r in range(2):
                    self_keep(l, SELF - 2 + r, r)
                for r in range(2):
                    linear(l, NS + SELF - 2 + r, r, NS // J + SELF - 2 + r, r, 0)
                act.wait_ge(f_exp, l + 1)
                op.activation(gate[:, 0:2], gate[:, 0:2], ACT.Exp).then_inc(f_gate, 1)
                with act.Fori(0, SELF // 2) as i:
                    for r in range(2):
                        m = l * SELF + i * 2 + r
                        act.wait_ge(gt_done, AHEAD + m + 1)
                        act.wait_ge(o_done, AHEAD + m - 1)
                        op.copy(at[:, r, :, 0:2 * P], psum[0:99, 2 * r:2 * r + 2, 0:2 * P])
                        op.copy(at[0:66, r, :, 2 * P:3 * P], psum[0:66, 2 * r:2 * r + 2, 2 * P:3 * P]).then_inc(at_done, 1)
                act.wait_ge(n_var, l + 1)
                op.activation(hsum[:, 2, :], hsum[:, 2, :], ACT.Sqrt).then_inc(n_sqrt, 1)

            for counter in (hid_done, rb_done, ta_done, gk_done, oh1_done, abs1_done):
                act.sem_inc(counter, AHEAD)
            act.wait_ge(ln_var, 1)
            op.activation(stat[:, 1, :], stat[:, 1, :], ACT.Sqrt).then_inc(ln_sqrt, 1)
            act.wait_ge(ln_var, 2)
            op.activation(norm[:, 0], norm[:, 0], ACT.Sqrt).then_inc(ln_sqrt, 1)
            act.wait_ge(l1_go, 1)

            def hidden(k, s, t):
                act.wait_ge(wbl[s // 3], 16 * t + 16)
                act.wait_ge(rr_done, AHEAD + k - 1)
                op.activation(hid[0:64, s % 2, :], wb[:, s, :], ACT.Relu, bias=w1c[:, 1:2], scale=w1c[:, 0:1]).then_inc(hid_done, 1)

            def scalars(k, s, t):
                act.wait_ge(gat[s], 32 * (LAYERS * GROUPS * BODIES) + 32 * t + 32)
                act.wait_ge(mix_done, START + (k - 2) * OPS + 1)
                op.copy(ta[:, s % 2, :, 0:8], xg[:, s, :, 96:104]).then_inc(ta_done, 1)

            def matrices(k, half):
                act.wait_ge(mix_done, START + (k - 3) * OPS)
                r_ = unit[:, bass.ds(k, 3)].rearrange("p s e i -> p (s e) i")
                g_ = gk[:, half]
                op.copy(g_[:, :, :, 0], r_)
                for o, i, c, sign in ((0, 1, 2, -1), (0, 2, 1, 1), (1, 0, 2, 1), (1, 2, 0, -1), (2, 0, 1, -1), (2, 1, 0, 1)):
                    last = op.mul(g_[:, :, o, 1 + i], r_[:, :, c], float(sign))
                last.then_inc(gk_done, 1)

            def one_hot1(k, r):
                act.wait_ge(ag1_done, AHEAD + k - 1)
                act.wait_ge(oh1_done, AHEAD + k)
                for e in range(2):
                    last = op.activation(dist[:, e, :], iota_f[:], ACT.Abs, bias=ndloc[:, bass.ds(k, 1), e])
                last.then_inc(abs1_done, 1)
                act.wait_ge(abs1_done, AHEAD + k + 1)
                op.activation(oh[:, r], dist[:], ACT.Relu, bias=1.0, scale=-1.0).then_inc(oh1_done, 1)

            def radial_out(k, r):
                act.wait_ge(rr_done, AHEAD + k + 1)
                act.wait_ge(pb_done, AHEAD + k - 1)
                act.wait_ge(mix_done, START + (k - 2) * OPS + 5)
                op.copy(rb[:, r].rearrange("p e c -> p (e c)"), psum[:, 4 + r, 0:2 * P]).then_inc(rb_done, 1)

            hidden(0, 0, 0)
            hidden(1, 1, 0)
            scalars(0, 0, 0)
            radial_out(0, 0)
            with act.Fori(0, NS // S6 - 1) as i:
                for s in range(S6):
                    k = i * S6 + s
                    if s % 3 == 0:
                        matrices(k, s // 3)
                    one_hot1(k, s % 2)
                    hidden(k + 2, (s + 2) % S6, i + (s + 2) // S6)
                    radial_out(k + 1, (s + 1) % 2)
                    scalars(k + 1, (s + 1) % S6, i + (s + 1) // S6)
            for s in range(S6):
                k, i = NS - S6 + s, NS // S6 - 1
                if s % 3 == 0:
                    matrices(k, s // 3)
                one_hot1(k, s % 2)
                if s + 2 < S6:
                    hidden(k + 2, s + 2, i)
                if s + 1 < S6:
                    radial_out(k + 1, (s + 1) % 2)
                    scalars(k + 1, s + 1, i)
            act.wait_ge(ln_var, 3)
            op.activation(stat[:, 1, :], stat[:, 1, :], ACT.Sqrt).then_inc(ln_sqrt, 1)

        @block.vector
        def _(v):
            op = nc.vector

            def seq(instruction):
                v.drain()
                return instruction

            op.memset(ones[:], 1.0)
            op.memset(ones_b[:], 1.0)
            op.memset(bz[:], 0.0)
            op.memset(zero1[:], -2.0)
            op.memset(cnt, 0.0)
            op.memset(xn[:, BLOCKS:NB, :], 0.0)
            v.wait_ge(s_iota, 6)
            op.tensor_scalar(ident[:], iota_f[:], iota_p[:, 0:1], None, ALU.is_equal)
            op.tensor_scalar(part_i[:, 1:2], part_i[:, 0:1], 7, None, ALU.bitwise_and)
            op.tensor_scalar(tci[:, 0:1], part_i[:, 0:1], 3, None, ALU.logical_shift_right)
            seq(None)
            op.tensor_copy(part_f[:, 0:1], part_i[:, 1:2])
            op.tensor_copy(part_f[:, 1:2], tci[:, 0:1])
            seq(None)
            op.tensor_scalar(mask_c[:], iota_f[:, 0:CH], part_f[:, 1:2], None, ALU.is_equal)
            op.tensor_scalar(sel_h[:], iota_f[:, 0:H], part_f[:, 0:1], None, ALU.is_equal)
            op.tensor_scalar(iota_i, iota_i, 7, None, ALU.bitwise_and)
            seq(None)
            op.tensor_copy(below[0:H, 0:P], iota_i[0:H, :])
            seq(None)
            op.tensor_scalar(sel_ht[:], below[0:H, 0:P], iota_p[0:H, 0:1], None, ALU.is_equal)

            v.wait_ge(s_in, 32)
            op.tensor_copy(dstf, dsti)
            seq(None)
            for b in range(1, BLOCKS + 1):
                seq(op.tensor_scalar(below, dstf, float(b * P), None, ALU.is_lt, ALU.add, accum_out=cnt[:, b:b + 1]))
            v.sem_inc(s_set, 1)
            v.wait_ge(s_pe, 1)
            r = lambda k, a=0, b=NB: rowf[:, k, a:b]
            ri = lambda k, a=0, b=NB: rowi[:, k, a:b]
            seq(op.tensor_copy(r(0), psum[0:1, 0, 0:NB]))
            op.tensor_copy(ri(0), r(0))
            seq(op.tensor_scalar(r(1), r(0), -1.0, None, ALU.add))
            op.tensor_scalar(ri(0), ri(0), 8, None, ALU.arith_shift_right)
            seq(op.tensor_copy(ri(1), r(1)))
            op.tensor_copy(r(2), ri(0))
            seq(op.tensor_scalar(ri(1), ri(1), 8, None, ALU.arith_shift_right))
            seq(op.tensor_copy(r(3), ri(1)))
            op.tensor_tensor(r(4, 0, BLOCKS), r(3, 1, BLOCKS + 1), r(2, 0, BLOCKS), ALU.subtract)
            seq(op.tensor_tensor(r(5, 0, BLOCKS), r(0, 1, BLOCKS + 1), r(0, 0, BLOCKS), ALU.is_gt))
            seq(op.scalar_tensor_tensor(r(6, 0, BLOCKS), r(4, 0, BLOCKS), 1.0, r(5, 0, BLOCKS), ALU.add, ALU.mult))
            seq(op.memset(r(10), 0.0))
            seq(op.tensor_tensor_scan(r(7, 0, BLOCKS), r(10, 0, BLOCKS), r(6, 0, BLOCKS), 0.0, ALU.add, ALU.add))
            seq(op.tensor_tensor(r(8, 0, BLOCKS), r(7, 0, BLOCKS), r(6, 0, BLOCKS), ALU.subtract))
            seq(op.tensor_tensor(r(11, 0, BLOCKS), r(2, 0, BLOCKS), r(8, 0, BLOCKS), ALU.subtract))
            seq(op.tensor_tensor(r(9, 1, BLOCKS), r(11, 1, BLOCKS), r(11, 0, BLOCKS - 1), ALU.subtract))
            v.sem_inc(s_set, 1)
            v.wait_ge(s_pe, 2)
            op.memset(rd[:, 0:1], 1.0)
            op.tensor_copy(rd[:, 1:2], psum[0:BLOCKS - 1, 1, 1:2])
            seq(op.tensor_copy(col, psum[0:BLOCKS - 1, 1, 0:2]))
            seq(op.tensor_scalar(mask, iota_k[0:BLOCKS - 1], col[:, 0:1], None, ALU.is_ge))
            v.sem_inc(s_set, 1)
            v.wait_ge(s_pe, 3)
            steps = psum[:, 2, 0:2 * KQ].rearrange("p (q t) -> p q t", t=2)
            op.tensor_copy(brow[:], psum[0:1, 3, 0:NSP])
            op.tensor_scalar(bcol, steps[:, :, 0], float(P), None, ALU.mult)
            seq(op.tensor_tensor(tcol, kcol, steps[:, :, 1], ALU.add))
            seq(op.tensor_scalar(tcol, tcol, float(PAIRS), None, ALU.min))
            seq(op.tensor_copy(tci, tcol))
            v.sem_inc(s_set, 1)

            v.wait_ge(s_wt, 16 * WEIGHT_LOADS)
            seq(op.tensor_tensor(bsum.rearrange("p (l z) -> p l z", l=LAYERS)[0:96, :, 0:HC],
                                 bsum.rearrange("p (l z) -> p l z", l=LAYERS)[0:96, :, 0:HC],
                                 bsum2.rearrange("p (l z) -> p l z", l=LAYERS)[0:96, :, 0:HC], ALU.add))
            for w, parts in ((wz[:], P), (bsum.rearrange("p (l z) -> p l z", l=LAYERS), 96)):
                seq(op.tensor_tensor(wtmp[0:parts].rearrange("p (l k) -> p l k", l=LAYERS), w[0:parts, :, 0:HC],
                                     watt[0:parts].rearrange("p (l k) -> p l k", l=LAYERS), ALU.mult))
                seq(op.tensor_reduce(wlin[0:parts], wtmp[0:parts].rearrange("p (k c) -> p k c", c=C), AX.X, ALU.add))
                seq(op.tensor_scalar(w[0:parts, :, HC:ZW], wlin[0:parts].rearrange("p (l h) -> p l h", l=LAYERS),
                                     NSLOPE, None, ALU.mult))
            op.tensor_scalar(atts[:].rearrange("p l k -> p (l k)"), watt, 1.0 - NSLOPE, None, ALU.mult)
            for part in range(3):
                seq(op.tensor_copy(bhb[0:96], bsum[0:96]))
                op.tensor_copy(bz[32 * part:32 * part + 1].rearrange("p l z -> p (l z)"), bhb[32 * part:32 * part + 1])
                seq(op.tensor_tensor(bsum[0:96], bsum[0:96], bhb[0:96], ALU.subtract))

            v.wait_ge(s_rows, 16 * 2 * KQ)
            seq(op.tensor_copy(srcf, drow))
            for q in range(KQ):
                op.tensor_scalar(dl[:, q, :], srcf[:, q, :], bcol[:, q:q + 1], None, ALU.subtract)
            seq(None)
            seq(op.tensor_scalar(dl, dl, -1.0, float(P), ALU.max, ALU.min))
            op.tensor_scalar(valid, dl, 0.0, None, ALU.is_ge)
            op.tensor_copy(dlb[:], dl)
            seq(None)
            seq(op.scalar_tensor_tensor(valid, dl, float(P), valid, ALU.is_lt, ALU.mult))
            seq(op.scalar_tensor_tensor(key, srcf, 1.0, valid, ALU.add, ALU.mult))
            seq(op.tensor_scalar(key, key, -1.0, None, ALU.add))
            v.sem_inc(s_set, 1)
            seq(op.tensor_scalar(drow, srow, P - 1, None, ALU.bitwise_and))
            seq(op.tensor_scalar(srow, srow, 7, None, ALU.logical_shift_right))
            op.scalar_tensor_tensor(srcf, drow, float(BLOCKS), srow, ALU.mult, ALU.add)
            v.wait_ge(s_kw, 16 * (KQ + 1))
            op.tensor_copy(first[:], firstb[:])
            op.tensor_scalar(valid, kw[:, :, 1:PAIR + 1], 0.0, None, ALU.is_ge)
            seq(op.tensor_tensor(lastr, kw[:, :, 1:PAIR + 1], kw[:, :, 2:PAIR + 2], ALU.not_equal))
            seq(op.tensor_tensor(lastr, lastr, valid, ALU.mult))
            v.sem_inc(s_set, 1)
            for k in range(2 * KQ):
                q, e = k // 2, k % 2
                n = slice(q * P, q * P + P)
                v.wait_ge(s_tr, k + 1)
                three = psum[:, 4 + 2 * e, :]
                op.tensor_copy(srci[:, n, e], three[:, 0:P])
                op.tensor_scalar(ndloc[:, n, e], three[:, P:2 * P], -1.0, None, ALU.mult)
                op.tensor_copy(laste[:, n, e], three[:, 2 * P:3 * P])
                seq(op.tensor_copy(vedge[:, n, e, :], psum[:, 5 + 2 * e, 0:3 * P].rearrange("p (f k) -> p k f", f=3)))
                v.sem_inc(s_trc, 1)
            v.sem_inc(s_ready, 1)

            for g in range(GROUPS):
                kwin = kwins[g % 2]
                v.wait_ge(s_win[g % 2], 16 * (g // 2 + 1))
                seq(op.tensor_tensor(run_f[:, 0:CW], kwin[:, 0:CW], kwin[:, 1:CW + 1], ALU.not_equal))
                seq(op.tensor_tensor(run_b[:, 0:1], kwin[:, CW:CW + 1], kwin[:, CW + 1:CW + 2], ALU.not_equal))
                v.sem_inc(s_flag, 1)
                if g > 0:
                    v.wait_ge(s_flst, 16 * g)
                op.tensor_scalar(fl[:, 0:CW], run_f[:, 0:CW], -BIG, None, ALU.mult)
                seq(op.tensor_scalar(fl[:, CW:CW + 1], run_b[:, 0:1], -BIG, None, ALU.mult))
                op.tensor_tensor_scan(fl[:, CW + 1:2 * CW + 1], fl[:, 0:CW], fl[:, 0:CW], 0.0, ALU.min, ALU.min)
                seq(op.tensor_tensor_scan(fl[:, 2 * CW + 1:3 * CW + 1][:, ::-1], fl[:, 1:CW + 1][:, ::-1],
                                          fl[:, 1:CW + 1][:, ::-1], 0.0, ALU.min, ALU.min))
                v.sem_inc(s_flag, 1)

            op.memset(xs[:, :, :, :, C:C1], 1.0)
            op.memset(xw[:], 0.0)
            op.memset(carry[:], -BIG)
            op.memset(slope[:], 0.01)
            op.memset(real[:], 1.0)
            seq(None)
            op.memset(slope[:, 2:3], 1.0)
            op.memset(real[:, BLOCKS - 1:NB], 0.0)
            seq(None)
            op.tensor_scalar(real[:, BLOCKS - 1:BLOCKS], iota_p[:], float(N - (BLOCKS - 1) * P), None, ALU.is_lt)
            for counter in (u_done, r_done, l_done, oht_done, px_done, acc_done, gb_done, h_done):
                v.sem_inc(counter, AHEAD)
            v.sem_inc(c_end, 1)
            v.wait_ge(s_flst, 16 * GROUPS)
            seq(None)
            v.sem_inc(s_ready, 1)

            def one_hot_t(l, g, i, k, s):
                v.wait_ge(drl[s // 3 % 2], 16 * ((l * GROUPS + g) * BODIES + i + s // S6) + 16)
                v.wait_ge(front_done, AHEAD + l * ZS + k - 1)
                op.tensor_scalar(oht[:, s % 2, :], dr[:, s % S6, :], iota_p[:, 0:1], None, ALU.is_equal).then_inc(oht_done, 1)

            def weighted(l, n, r):
                v.wait_ge(z_done, AHEAD + l * ZS + n + 1)
                v.wait_ge(r_done, AHEAD + l * ZS + n - 1)
                op.scalar_tensor_tensor(
                    u[:, r], z_ps(r, 0, HC), 0.0,
                    atts[:, bass.ds(l, 1), :].to_broadcast([P, 2, HC]), ALU.max, ALU.mult).then_inc(u_done, 1)

            def over_channels(l, n, r, q, c, j):
                v.wait_ge(u_done, AHEAD + l * ZS + n + 1)
                if j == 0:
                    v.wait_ge(l_done, AHEAD + l * QS + q - 1)
                op.tensor_reduce(lr[:, c, j], u[:, r].rearrange("p e (h c) -> p e h c", h=H), AX.X, ALU.add).then_inc(r_done, 1)

            def logits(l, n, c, steps, to):
                v.wait_ge(r_done, AHEAD + l * ZS + n + 1)
                v.wait_ge(lin_done, AHEAD + l * ZS + n + 1)
                op.tensor_tensor(to, lr[:, c, 0:steps].rearrange("p j e h -> p (j e) h"),
                                 lin[:, c, 0:steps].rearrange("p j e h -> p (j e) h"), ALU.add).then_inc(l_done, 1)

            def chunk_logits(l, g, i, half):
                n = ((g * BODIES + i) * 2 + half) * J + J - 1
                logits(l, n, half, J, lg[:, :, bass.ds(i * 2 + half, 1), :].rearrange("p k o h -> p (k o) h"))

            def weigh_rows(l, g, i, k, s):
                r, c, j = s % 2, i * 2 + s // J, s % J
                m = l * NS + k
                v.wait_ge(xs_done, AHEAD + m + 1)
                v.wait_ge(agg_done, AHEAD + m - 1)
                rows = xs[:, bass.ds((l * GROUPS + g) % 2, 1), bass.ds(i * S6 + s, 1), :, :].rearrange("p o q e c -> p (o q e) c")
                op.tensor_tensor(
                    px[:, r, :, 0:H * C1].rearrange("p e (h c) -> p e h c", h=H),
                    rows.unsqueeze(2).to_broadcast([P, 2, H, C1]),
                    pg[:, 2 * j:2 * j + 2, bass.ds(c, 1), :].rearrange("p e o h -> p e (o h)").unsqueeze(3).to_broadcast([P, 2, H, C1]),
                    ALU.mult).then_inc(px_done, 1)

            def add_sums(l, g, k, r):
                b = v.value_load(brow[0:1, bass.ds(k, 1)], min_val=0, max_val=BLOCKS - 1)
                v.wait_ge(agg_done, AHEAD + l * NS + k + 1)
                v.wait_ge(acc_done, AHEAD + l * AGGS + 2 + g + k)
                sums = acc[:, bass.ds(b, 1), :].rearrange("p o a -> p (o a)")
                op.tensor_tensor(sums, sums, agg_ps(r), ALU.add).then_inc(acc_done, 1)

            def dve_body(l, g, i, a, b, starts_group, ends_group):
                k0 = (g * BODIES + i) * S6
                for s in range(S6):
                    r = s % 2
                    if b:
                        weigh_rows(l, g - 1, i, k0 - GS + s, s)
                    if a and s == J:
                        chunk_logits(l, g, i, 0)
                    if a and s == 0 and not starts_group:
                        chunk_logits(l, g, i - 1, 1)
                    if a and (s + 3 < S6 or not ends_group):
                        one_hot_t(l, g, i, k0 + s + 3, s + 3)
                    if a:
                        weighted(l, k0 + s, r)
                    if b and (s > 0 or not starts_group):
                        add_sums(l, g - 1, k0 - GS + s - 1, 1 - r)
                    if a:
                        over_channels(l, k0 + s, r, (g * BODIES + i) * 2 + s // J, s // J, s % J)

            def dve_group(l, g, a, b):
                if a:
                    for s in range(3):
                        one_hot_t(l, g, 0, g * GS + s, s)
                dve_body(l, g, 0, a, b, True, False)
                with v.Fori(1, BODIES - 1) as i:
                    dve_body(l, g, i, a, b, False, False)
                dve_body(l, g, BODIES - 1, a, b, False, True)
                if a:
                    chunk_logits(l, g, BODIES - 1, 1)
                if b:
                    add_sums(l, g - 1, g * GS - 1, 1)

            def maxima(l, g, starts):
                q = l * GROUPS + g
                v.wait_ge(c_lt, q + 1)
                v.wait_ge(fl_done, 16 * q + 16)
                op.tensor_tensor_scan(run_f[:], fl[:, 0:CW], lt_ps, -BIG, ALU.add, ALU.max)
                seq(op.tensor_tensor_scan(run_b[:, ::-1], fl[:, 1:CW + 1][:, ::-1], lt_ps[:, ::-1], -BIG, ALU.add, ALU.max))
                open_f, open_b = fl[:, CW + 1:2 * CW + 1], fl[:, 2 * CW + 1:3 * CW + 1]
                op.tensor_scalar(ends[:, 0, :], mask_c[:], run_f[:, CW - 1:CW], None, ALU.mult)
                op.tensor_scalar(ends[:, 1, :], mask_c[:], run_b[:, 0:1], None, ALU.mult)
                op.tensor_scalar(ends[:, 2, :], mask_c[:], open_f[:, CW - 1:CW], None, ALU.mult)
                seq(op.tensor_scalar(ends[:, 3, :], mask_c[:], open_b[:, 0:1], None, ALU.mult))
                v.sem_inc(c_ends, 1)
                op.tensor_tensor(run_f[:], run_f[:], run_b[:], ALU.max)
                v.wait_ge(c_ch, q + 1)
                op.tensor_copy(chain[:].rearrange("p a c -> p (a c)"), psum[0:H, 6, 0:4 * CH])
                if starts:
                    op.memset(carry[:, 0, 0:1], -BIG)
                else:
                    op.tensor_copy(carry[:, 0, 0:1], carry[:, 0, CH:CH + 1])
                seq(None)
                op.tensor_tensor_scan(carry[:, 0, 1:CH + 1], chain[:, 2, :], chain[:, 0, :], carry[:, 0, 0:1], ALU.add, ALU.max)
                seq(op.tensor_tensor_scan(carry[:, 1, 0:CH - 1][:, ::-1], chain[:, 3, 1:CH][:, ::-1],
                                          chain[:, 1, 1:CH][:, ::-1], -BIG, ALU.add, ALU.max))
                v.sem_inc(c_car, 1)
                v.wait_ge(c_bk, q + 1)
                seq(op.tensor_tensor(back[:], psum[:, 7, 0:2 * CH].rearrange("p (a c) -> p a c", a=2),
                                     mask_c[:].unsqueeze(1).to_broadcast([P, 2, CH]), ALU.mult))
                seq(op.tensor_reduce(carried[:], back[:], AX.X, ALU.add))
                seq(op.scalar_tensor_tensor(run_f[:], open_f, carried[:, 0:1], run_f[:], ALU.add, ALU.max))
                seq(op.scalar_tensor_tensor(run_f[:], open_b, carried[:, 1:2], run_f[:], ALU.add, ALU.max))
                v.sem_inc(c_t, 1)
                op.tensor_scalar(fix[:, 0:1], open_f[0:H, 0:1], 0.0, None, ALU.is_ge)
                op.tensor_scalar(fhot[:], iota_f[0:H, :], first[:, bass.ds(g, 1)], None, ALU.is_equal)
                seq(op.tensor_tensor(fix[:, 1:2], carried[0:H, 0:1], run_f[0:H, 0:1], ALU.subtract))
                seq(op.tensor_tensor(fix[:, 1:2], fix[:, 1:2], fix[:, 0:1], ALU.mult))
                v.sem_inc(c_fx, 1)
                v.wait_ge(c_fe, q + 1)
                seq(op.tensor_scalar(fix[:, 3:4], fix[:, 2:3], -1.0, None, ALU.add))
                seq(op.tensor_scalar(fixd[:], ident[0:H, 0:H], fix[:, 3:4], None, ALU.mult))
                v.sem_inc(c_fd, 1)
                v.wait_ge(c_tp, q + 1)
                seq(op.tensor_tensor(lg[:].rearrange("p k c h -> p (k c h)"), lg[:].rearrange("p k c h -> p (k c h)"),
                                     tp_ps, ALU.subtract))
                v.sem_inc(c_sub, 1)
                for j in range(J):
                    lasts = laste[:, bass.ds(g * GS, GS), :].rearrange("p (c j) e -> p j e c", j=J)[:, j]
                    op.tensor_tensor(mg[:, 2 * j:2 * j + 2],
                                     tp_ps[:, 2 * j * P:(2 * j + 2) * P].rearrange("p (e c h) -> p e c h", e=2, c=CH),
                                     lasts.unsqueeze(3).to_broadcast([P, 2, CH, H]), ALU.mult)
                v.wait_ge(c_fn, q + 1)
                seq(op.tensor_scalar(fixn[:], psum[:, 6, 0:H], 1.0, None, ALU.add))
                b = v.value_load(brow[0:1, bass.ds(g * GS, 1)], min_val=0, max_val=BLOCKS - 1)
                v.wait_ge(acc_done, AHEAD + l * AGGS + 1 + g * (GS + 1))
                sums = acc[:, bass.ds(b, 1), 0:H * C1].rearrange("p o (h c) -> p (o h) c", h=H)
                op.tensor_tensor(sums, sums, fixn[:].unsqueeze(2).to_broadcast([P, H, C1]), ALU.mult).then_inc(acc_done, 1)
                seq(None)
                v.wait_ge(c_pg, q + 1)
                v.sem_inc(c_end, 1)

            def blocks(m):
                return bass.ds(m * 2, 2) if not isinstance(m, int) else slice(m * 2, m * 2 + 2)

            def normalized(l, m, r):
                out_g = gb[:, r].rearrange("p b (h c) -> p b h c", h=H)
                v.wait_ge(gt_done, AHEAD + l * SELF + m - 1)
                seq(op.tensor_tensor(out_g, acc[:, blocks(m), 0:H * C1].rearrange("p b (h c) -> p b h c", h=H),
                                     gate[:, 2, blocks(m), :].unsqueeze(3).to_broadcast([P, 2, H, C1]), ALU.mult))
                v.wait_ge(xp_done, AHEAD + l * SELF + m + 1)
                op.tensor_tensor(out_g[:, :, :, 0:C], out_g[:, :, :, 0:C],
                                 xp[:, r].rearrange("p b (h c) -> p b h c", h=H), ALU.add)
                seq(op.tensor_tensor(out_g[:, :, :, C], out_g[:, :, :, C], gate[:, 3, blocks(m), :], ALU.add))
                v.sem_inc(gb_done, 1)

            def residual(l, m, r):
                v.wait_ge(o_done, AHEAD + l * SELF + m + 1)
                here = hn[:, blocks(m), :]
                seq(op.scalar_tensor_tensor(here, psum[:, 4 + r, 0:2 * C].rearrange("p (b c) -> p b c", b=2), 1.0 / H,
                                            cb[:, bass.ds(l, 1), :].to_broadcast([P, 2, C]), ALU.mult, ALU.add))
                seq(op.scalar_tensor_tensor(here, here, slope[:, bass.ds(l, 1)], here, ALU.mult, ALU.max))
                op.tensor_tensor(here, here, xn[:, blocks(m), :], ALU.add).then_inc(h_done, 1)

            with v.Fori(0, LAYERS) as l:
                v.sem_inc(x_new, 1)
                seq(op.tensor_copy(x3[:, :, 0:C], xn[:]))
                seq(op.tensor_tensor(hn[:], xn[:], x3[:, :, 0:C], ALU.subtract))
                seq(op.tensor_copy(x3[:, :, C:2 * C], hn[:]))
                seq(op.tensor_tensor(hn[:], hn[:], x3[:, :, C:2 * C], ALU.subtract))
                seq(op.tensor_copy(x3[:, :, 2 * C:3 * C], hn[:]))
                v.sem_inc(x3_new, 1)
                dve_group(l, 0, True, False)
                maxima(l, 0, True)
                with v.Fori(1, GROUPS) as g:
                    dve_group(l, g, True, True)
                    maxima(l, g, False)
                dve_group(l, GROUPS, False, True)

                with v.Fori(0, SELF // 2) as i:
                    for r in range(2):
                        weighted(l, NS + i * 2 + r, r)
                    for r in range(2):
                        over_channels(l, NS + i * 2 + r, r, NS // J + i * 2 + r, r, 0)
                    for r in range(2):
                        logits(l, NS + i * 2 + r, r, 1, self_l[:, bass.ds(i * 4 + 2 * r, 2), :])
                v.wait_ge(acc_done, AHEAD + (l + 1) * AGGS)
                v.wait_ge(l_done, AHEAD + (l + 1) * QS)
                sums = acc[:, :, 0:H * C1].rearrange("p b (h c) -> p b h c", h=H)
                den, top = sums[:, :, :, C], acc[:, :, H * C1:AGG]
                g0, g1, g2, g3 = (gate[:, k] for k in range(4))
                seq(op.tensor_scalar(g0, den, 0.0, -BIG, ALU.is_equal, ALU.mult))
                seq(op.tensor_tensor(g0, g0, top, ALU.add))
                seq(op.tensor_tensor(g2, g0, self_l[:], ALU.max))
                op.tensor_tensor(g0, g0, g2, ALU.subtract)
                seq(op.tensor_tensor(g1, self_l[:], g2, ALU.subtract))
                v.sem_inc(f_exp, 1)
                v.wait_ge(f_gate, l + 1)
                seq(op.tensor_tensor(g2, den, g0, ALU.mult))
                seq(op.scalar_tensor_tensor(g2, g1, 1e-16, g2, ALU.add, ALU.add))
                seq(op.reciprocal(g2, g2))
                op.tensor_tensor(g3, g1, g2, ALU.mult)
                seq(op.tensor_tensor(g2, g0, g2, ALU.mult))
                v.sem_inc(f_g, 1)
                normalized(l, 0, 0)
                with v.Fori(0, SELF // 2 - 1) as i:
                    for r in range(2):
                        normalized(l, i * 2 + r + 1, 1 - r)
                        residual(l, i * 2 + r, r)
                normalized(l, SELF - 1, 1)
                residual(l, SELF - 2, 0)
                residual(l, SELF - 1, 1)
                seq(None)
                mask_n = real[:].unsqueeze(2).to_broadcast([P, NB, C])
                seq(op.tensor_tensor(hn[:], hn[:], mask_n, ALU.mult))
                seq(op.tensor_reduce(hsum[:, 0, :], hn[:].rearrange("p b c -> p c b"), AX.X, ALU.add))
                v.sem_inc(n_sum, 1)
                v.wait_ge(n_all, 2 * l + 1)
                seq(op.tensor_scalar(hsum[:, 3, :], psum[:, 6, 0:C], 1.0 / N, None, ALU.mult))
                seq(op.tensor_tensor(hn[:], hn[:], hsum[:, 3:4, :].to_broadcast([P, NB, C]), ALU.subtract))
                seq(op.tensor_tensor(hn[:], hn[:], mask_n, ALU.mult))
                seq(op.tensor_tensor(xn[:], hn[:], hn[:], ALU.mult))
                seq(op.tensor_reduce(hsum[:, 1, :], xn[:].rearrange("p b c -> p c b"), AX.X, ALU.add))
                v.sem_inc(n_sum, 1)
                v.wait_ge(n_all, 2 * l + 2)
                seq(op.tensor_scalar(hsum[:, 2, :], psum[:, 7, 0:C], 1.0 / N, EPS, ALU.mult, ALU.add))
                v.sem_inc(n_var, 1)
                v.wait_ge(n_sqrt, l + 1)
                seq(op.reciprocal(hsum[:, 3, :], hsum[:, 2, :]))
                seq(op.tensor_tensor(hsum[:, 3, :], hsum[:, 3, :], gm[:, bass.ds(l, 1), :].rearrange("p o c -> p (o c)"), ALU.mult))
                seq(op.tensor_tensor(hn[:], hn[:], hsum[:, 3:4, :].to_broadcast([P, NB, C]), ALU.mult))
                seq(op.tensor_tensor(xn[:], hn[:], bt[:, bass.ds(l, 1), :].to_broadcast([P, NB, C]), ALU.add))
            v.sem_inc(x_new, 1)

            def layer_norm(a, b, count):
                m_, s_ = stat[:, 0, :], stat[:, 1, :]
                wide = lambda t: t.unsqueeze(2).to_broadcast([P, NB, C])
                seq(op.tensor_tensor(hn[:], a, b, ALU.add))
                seq(op.tensor_reduce(m_, hn[:], AX.X, ALU.add))
                seq(op.tensor_scalar(m_, m_, 1.0 / C, None, ALU.mult))
                seq(op.tensor_tensor(hn[:], hn[:], wide(m_), ALU.subtract))
                seq(op.tensor_tensor(xn[:], hn[:], hn[:], ALU.mult))
                seq(op.tensor_reduce(s_, xn[:], AX.X, ALU.add))
                seq(op.tensor_scalar(s_, s_, 1.0 / C, EPS, ALU.mult, ALU.add))
                v.sem_inc(ln_var, 1)
                v.wait_ge(ln_sqrt, count)
                seq(op.reciprocal(s_, s_))
                seq(op.tensor_tensor(xn[:], hn[:], wide(s_), ALU.mult))
                v.sem_inc(x_new, 1)

            v.wait_ge(x0_in, 16)
            layer_norm(hn[:], xn[:], 1)

            v.wait_ge(v_in, 16 * 5)
            edges = vec[:, 0:NS]
            seq(op.tensor_tensor(unit, edges, edges, ALU.mult))
            seq(op.tensor_reduce(norm[:, 0], unit, AX.X, ALU.add))
            v.sem_inc(ln_var, 1)
            y0, c1 = 0.5 / sqrt(pi), sqrt(3.0 / (4.0 * pi))
            n0 = sqrt(4.0 * pi) / sqrt(2 * 8)
            n1 = sqrt(4.0 * pi) * sqrt(3.0) / sqrt(8 + 8 * 3)
            third, beta2 = 1.0 / sqrt(3.0), n1 * sqrt(3.0 / (8.0 * pi))
            raw = w2raw.rearrange("q (g u v) -> q g u v", u=8, v=8)
            raw11 = w2raw[:, 192:384].rearrange("q (u v k) -> q u v k", v=8, k=3)
            wa = w2e[:, 0:256].rearrange("q (u t) -> q u t", t=16)
            wbd = w2e[:, 256:384].rearrange("q (u v) -> q u v", v=8)
            op.tensor_scalar(wa[:, 0:8, 0:8], raw[:, 0], n0 * y0, None, ALU.mult)
            op.tensor_scalar(wa[:, 0:8, 8:16], raw[:, 1], n0 * c1 * third, None, ALU.mult)
            op.tensor_scalar(wa[:, 8:16, 0:8], raw[:, 2], n1 * c1 * third, None, ALU.mult)
            op.tensor_scalar(wa[:, 8:16, 8:16], raw11[:, :, :, 2], beta2, None, ALU.mult)
            op.tensor_scalar(wbd[:, 8:16], raw11[:, :, :, 1], n1 * c1 / sqrt(6.0), None, ALU.mult)
            seq(op.tensor_scalar(wbd[:, 0:8], raw11[:, :, :, 0], n1 * y0 * third, None, ALU.mult))
            op.scalar_tensor_tensor(wbd[:, 0:8], raw11[:, :, :, 2], -beta2 / 3.0, wbd[:, 0:8], ALU.mult, ALU.add)
            op.memset(acc1, 0.0)
            op.memset(gk, 0.0)
            op.memset(hid[64:65, :, :], 1.0)
            v.wait_ge(ln_sqrt, 2)
            seq(op.reciprocal(norm[:, 1], norm[:, 0]))
            for i, c in enumerate((1, 2, 0)):
                op.tensor_tensor(unit[:, :, :, i], edges[:, :, :, c], norm[:, 1], ALU.mult)
            seq(None)
            v.sem_inc(mix_done, START)
            v.sem_inc(l1_go, 1)

            def vectors(s):
                return xg[:, s, :, 104:128].rearrange("p e (v i) -> p e v i", i=3)

            def dot(k, s, t):
                v.wait_ge(gat[s], 32 * (LAYERS * GROUPS * BODIES) + 32 * t + 32)
                return op.tensor_tensor(sprod[:, s % 2].rearrange("p e (v i) -> p e v i", i=3), vectors(s),
                                        unit[:, bass.ds(k, 1)].rearrange("p o e i -> p (o e) i").unsqueeze(2).to_broadcast([P, 2, 8, 3]),
                                        ALU.mult)

            def dots(s):
                return op.tensor_reduce(ta[:, s % 2, :, 8:16], sprod[:, s % 2].rearrange("p e (v i) -> p e v i", i=3), AX.X, ALU.add)

            def add_messages(k, r):
                b = v.value_load(brow[0:1, bass.ds(k, 1)], min_val=0, max_val=BLOCKS - 1)
                v.wait_ge(ag1_done, AHEAD + k + 1)
                v.wait_ge(mix_done, START + (k + 1) * OPS + 7)
                sums = acc1[:, bass.ds(b, 1), :].rearrange("p o c -> p (o c)")
                return op.tensor_tensor(sums, sums, psum[:, 6 + r, 0:C], ALU.add)

            def messages(i, s, starts, ends):
                k, r = i * S6 + s, s % 2
                at_ = START + k * OPS
                v.wait_ge(rr_done, AHEAD + k + 1)
                v.wait_ge(ta_done, AHEAD + k + 1)
                v.wait_ge(mix_done, at_ - OPS + 4)
                op.tensor_tensor(pa[:, r].rearrange("p e (u t) -> p e u t", t=16),
                                 z_ps(r, 0, 256).rearrange("p e (u t) -> p e u t", t=16),
                                 ta[:, r].unsqueeze(2).to_broadcast([P, 2, 16, 16]), ALU.mult).then_inc(mix_done, 1)
                if ends:
                    v.wait_ge(mix_done, at_ + 1)
                    v.sem_inc(mix_done, 1)
                else:
                    dot(k + 1, (s + 1) % S6, i + (s + 1) // S6).then_inc(mix_done, 1)
                v.wait_ge(mix_done, at_ + 1)
                op.tensor_reduce(xo[:, r, :, 0, :], pa[:, r].rearrange("p e (u t) -> p e u t", t=16), AX.X, ALU.add).then_inc(mix_done, 1)
                if ends:
                    v.wait_ge(mix_done, at_ + 3)
                    v.sem_inc(mix_done, 1)
                else:
                    v.wait_ge(mix_done, at_ + 2)
                    dots((s + 1) % S6).then_inc(mix_done, 1)
                v.wait_ge(rb_done, AHEAD + k + 1)
                op.tensor_tensor(pb[:, r, 1].rearrange("p (i u v) -> p i u v", i=3, v=8)[:, 2],
                                 rb[:, r, 1].rearrange("p (u v) -> p u v", v=8),
                                 xg[:, s, 1, 104:128].rearrange("p (v i) -> p i v", i=3)[:, 2].unsqueeze(1).to_broadcast([P, 16, 8]),
                                 ALU.mult).then_inc(mix_done, 1)
                v.wait_ge(pb_done, AHEAD + k + 1)
                v.wait_ge(mix_done, at_ + 5)
                op.tensor_reduce(xo[:, r, :, 1:4, :].rearrange("p e i u -> p e (i u)"),
                                 pb[:, r].rearrange("p e (x v) -> p e x v", v=8), AX.X, ALU.add).then_inc(mix_done, 1)
                if starts:
                    v.wait_ge(mix_done, at_ + 6)
                    v.sem_inc(mix_done, 1)
                else:
                    add_messages(k - 2, r).then_inc(mix_done, 1)
                v.wait_ge(gk_done, AHEAD + i * 2 + s // 3 + 1)
                v.wait_ge(mix_done, at_ + 6)
                for e in range(2):
                    op.tensor_tensor(gp[:, r, e].rearrange("p u (o j) -> p u o j", j=4),
                                     xo[:, r, e, :, 8:16].rearrange("p j u -> p u j").unsqueeze(2).to_broadcast([P, 8, 3, 4]),
                                     gk[:, s // 3, 2 * (s % 3) + e].unsqueeze(1).to_broadcast([P, 8, 3, 4]),
                                     ALU.mult).then_inc(mix_done, 1)
                v.wait_ge(ag1_done, AHEAD + k - 1)
                op.tensor_copy(msg[:, r, :, 0:8], xo[:, r, :, 0, 0:8]).then_inc(mix_done, 1)
                v.wait_ge(mix_done, at_ + 9)
                op.tensor_reduce(mg1[:, r], gp[:, r].rearrange("p e u (o j) -> p e (u o) j", j=4), AX.X, ALU.add).then_inc(mix_done, 1)
                v.wait_ge(mix_done, at_ + 11)
                op.tensor_tensor(msg[:, r, :, 8:32].rearrange("p e (u o) -> p e u o", o=3),
                                 mg1[:, r].rearrange("p e (u o) -> p e u o", o=3),
                                 xo[:, r, :, 1:4, 0:8].rearrange("p e o u -> p e u o"), ALU.add).then_inc(mix_done, 1)

            seq(dot(0, 0, 0))
            seq(dots(0))
            for s in range(S6):
                messages(0, s, s < 2, False)
            with v.Fori(1, NS // S6 - 1) as i:
                for s in range(S6):
                    messages(i, s, False, False)
            for s in range(S6):
                messages(NS // S6 - 1, s, False, s == S6 - 1)
            v.wait_ge(mix_done, START + NS * OPS)
            for k in (NS - 2, NS - 1):
                v.wait_ge(ag1_done, AHEAD + k + 1)
                b = v.value_load(brow[0:1, k:k + 1], min_val=0, max_val=BLOCKS - 1)
                sums = acc1[:, bass.ds(b, 1), :].rearrange("p o c -> p (o c)")
                seq(op.tensor_tensor(sums, sums, psum[:, 6 + k % 2, 0:C], ALU.add))
            layer_norm(xn[:], acc1, 3)


_INS = ['x', 'src', 'dst', 'edge_weight', 'edge_attr_3', 'L0_gnn_Wl', 'L0_gnn_bl', 'L0_gnn_Wr', 'L0_gnn_br',
        'L0_gnn_att', 'L0_gnn_conv_bias', 'L0_gnn_bn_gamma', 'L0_gnn_bn_beta',
        'L1_gnn_w1', 'L1_gnn_b1', 'L1_gnn_w2', 'L1_gnn_b2']


def kernel(**inputs):
    import concourse.bacc as bacc
    from concourse.bass_utils import run_bass_kernel_spmd

    nc = bacc.Bacc("TRN2", target_bir_lowering=False, num_devices=1)
    arrays, args = {}, []
    for name in _INS:
        a = np.ascontiguousarray(inputs[name])
        if name == 'x':
            a = np.concatenate([a, np.zeros((BLOCKS * P - N, C), a.dtype)])
            a = np.ascontiguousarray(a.reshape(BLOCKS, P, C).transpose(1, 0, 2))
        elif a.shape[0] == E:
            a = a.reshape(E, -1)
            pad = np.full((ROWS * PAIR - E, a.shape[1]), NOWHERE if name == 'dst' else 1 if name == 'edge_attr_3' else 0, a.dtype)
            a = np.concatenate([a, pad]).reshape(ROWS, -1)
        arrays[name] = a
        args.append(nc.dram_tensor(name, a.shape, mybir.dt.from_np(a.dtype), kind="ExternalInput").ap())
    args.append(nc.dram_tensor("out", (P, BLOCKS, C), F32, kind="ExternalOutput").ap())
    gatv2_program(nc, *args)
    r = run_bass_kernel_spmd(nc, [arrays], core_ids=[0])
    got = r.results[0]["out"]
    return np.ascontiguousarray(np.asarray(got).transpose(1, 0, 2).reshape(BLOCKS * P, C)[:N])
```
